# Optimizing a Trainium2 kernel written in Bass

```python
import numpy as np
import jax
import jax.numpy as jnp

def _softmax(x, axis=-1):
    return jax.nn.softmax(x, axis=axis)

def _gelu(x):
    return jax.nn.gelu(x, approximate=True)

def _silu(x):
    return jax.nn.silu(x)

def _sigmoid(x):
    return jax.nn.sigmoid(x)

def _layernorm(x, axis=-1, eps=1e-05):
    m = jnp.mean(x, axis=axis, keepdims=True)
    v = jnp.var(x, axis=axis, keepdims=True)
    return (x - m) / jnp.sqrt(v + eps)

def _scatter_add(tgt, idx, src, axis=0):
    return tgt.at[idx].add(src)

def _segment_sum(src, seg, n):
    return jax.ops.segment_sum(src, seg, n)
kernel_name = 'mk_decoder_postln_d1_seqx_r8_951b7f'

def setup_inputs(seed: int=0):
    np.random.seed(seed)
    _w = jnp.asarray

    def _rec_inputs():
        import jax
        import jax.numpy as jnp
        _rk = jax.random.key(seed)
        x = -0.0002928 + 1 * jax.random.normal(jax.random.fold_in(_rk, 1), (32, 64, 256), jnp.float32)
        _lenS = 64 - jax.random.randint(jax.random.fold_in(_rk, 7), (32,), 0, max(1, 64 // 4) + 1, jnp.int32)
        _lenS2 = 64 - jax.random.randint(jax.random.fold_in(_rk, 8), (32,), 0, max(1, 64 // 4) + 1, jnp.int32)
        _ctx_512P = jax.random.normal(jax.random.fold_in(_rk, 11), (32, 16, 64), jnp.float32)
        _ctx_512c = jax.random.dirichlet(jax.random.fold_in(_rk, 511), 0.3 * jnp.ones((16,), jnp.float32), (32, 64))
        _ctx_512t = jnp.einsum('bsk,bkd->bsd', _ctx_512c, _ctx_512P)
        _ctx_512t = _ctx_512t * jax.lax.rsqrt(jnp.mean(jnp.square(_ctx_512t)) + 1e-12) * 0.953939
        ctx_512 = 0.000227908 + 0.99994 * (_ctx_512t + 0.3 * jax.random.normal(jax.random.fold_in(_rk, 611), (32, 64, 64), jnp.float32))
        return (x, ctx_512)
    x, ctx_512 = _rec_inputs()

    def _L0_attn_setup():
        import jax, jax.numpy as jnp
        import numpy as np
        B, N, D, BS = (2, 512, 256, 32)

        def rms_norm(x):
            eps = jnp.asarray(jnp.finfo(x.dtype).eps, x.dtype)
            return x * jax.lax.rsqrt(jnp.mean(x * x, axis=-1, keepdims=True) + eps)

        def la_kernel(q, k, v, bs):
            b, n, d = q.shape
            T = n // bs
            qc = q.reshape(b, T, bs, d).transpose(1, 0, 2, 3)
            kc = k.reshape(b, T, bs, d).transpose(1, 0, 2, 3)
            vc = v.reshape(b, T, bs, d).transpose(1, 0, 2, 3)
            mask = jnp.tril(jnp.ones((bs, bs), q.dtype))

            def step(kv, qkv):
                qt, kt, vt = qkv
                s = jnp.einsum('bid,bjd->bij', qt, kt) * mask
                ot = jnp.einsum('bij,bjd->bid', s, vt) + jnp.einsum('bid,bde->bie', qt, kv)
                kv = kv + jnp.einsum('bjd,bje->bde', kt, vt)
                return (kv, ot)
            kv0 = jnp.zeros((b, d, d), q.dtype)
            _, o = jax.lax.scan(step, kv0, (qc, kc, vc))
            return o.transpose(1, 0, 2, 3).reshape(b, n, d)
        key = jax.random.key(seed)
        ks = jax.random.split(key, 6)
        scale = 0.02
        x = jax.random.normal(ks[0], (B, N, D), jnp.float32)
        Wq = jax.random.normal(ks[1], (D, D), jnp.float32) * scale
        Wk = jax.random.normal(ks[2], (D, D), jnp.float32) * scale
        Wv = jax.random.normal(ks[3], (D, D), jnp.float32) * scale
        Wg = jax.random.normal(ks[4], (D, D), jnp.float32) * scale
        Wp = jax.random.normal(ks[5], (D, D), jnp.float32) * scale
        return {'x': x, 'Wq': Wq, 'Wk': Wk, 'Wv': Wv, 'Wg': Wg, 'Wp': Wp}
    _L0_attn_all = _L0_attn_setup()
    _L0_attn_in = {k: v for k, v in _L0_attn_all.items() if k in ('Wq', 'Wk', 'Wv', 'Wg', 'Wp')}
    del _L0_attn_all

    def _L0_xattn_setup():
        import jax, jax.numpy as jnp
        import numpy as np
        B, S, L = (2, 128, 128)
        DIM_Q, H, K, D_C, D_CQ, R = (256, 16, 128, 64, 192, 64)

        def _rope_tables(length, dim):
            inv = 1.0 / 10000.0 ** (jnp.arange(0, dim, 2, dtype=jnp.float32) / dim)
            f = jnp.arange(length, dtype=jnp.float32)[:, None] * inv[None, :]
            sin = jnp.repeat(jnp.sin(f), 2, axis=-1)
            cos = jnp.repeat(jnp.cos(f), 2, axis=-1)
            return (sin, cos)

        def _rotate_half(x):
            half = x.shape[-1] // 2
            return jnp.concatenate([-x[..., half:], x[..., :half]], axis=-1)

        def _apply_rope(x, sin, cos):
            return x * cos + _rotate_half(x) * sin
        key = jax.random.key(seed)
        ks = jax.random.split(key, 8)
        return {'hidden_q': jax.random.normal(ks[0], (B, S, DIM_Q), jnp.float32), 'kv_c': jax.random.normal(ks[1], (B, L, D_C), jnp.float32), 'Wq': jax.random.normal(ks[2], (H * K, DIM_Q), jnp.float32) / np.sqrt(DIM_Q).astype(np.float32), 'w_kc_q': jax.random.normal(ks[3], (H, K, D_CQ), jnp.float32) / np.sqrt(K).astype(np.float32), 'w_kc_kv': jax.random.normal(ks[4], (H, K, D_C), jnp.float32) / np.sqrt(K).astype(np.float32), 'W_qr': jax.random.normal(ks[5], (H, D_CQ, R), jnp.float32) / np.float32(np.sqrt(D_CQ) * np.sqrt(R)), 'W_kr': jax.random.normal(ks[6], (H, D_C, R), jnp.float32) / np.sqrt(D_C).astype(np.float32), 'Wo': jax.random.normal(ks[7], (DIM_Q, H * K), jnp.float32) / np.sqrt(H * K).astype(np.float32)}
    _L0_xattn_all = _L0_xattn_setup()
    _L0_xattn_in = {k: v for k, v in _L0_xattn_all.items() if k in ('Wq', 'w_kc_q', 'w_kc_kv', 'W_qr', 'W_kr', 'Wo')}
    del _L0_xattn_all

    def _L0_ffn_setup():
        import jax
        import jax.numpy as jnp
        import numpy as np
        NUM_EXPERTS = 32
        HIDDEN = 256
        INTER = 96
        TOP_K = 8
        TAU = 0.05
        BATCH, SEQ = (2, 128)
        key = jax.random.key(seed)
        k1, k2, k3, k4 = jax.random.split(key, 4)
        return {'hidden_states': jax.random.normal(k1, (BATCH, SEQ, HIDDEN), dtype=jnp.float32), 'gate_weight': jax.random.normal(k2, (NUM_EXPERTS, HIDDEN), dtype=jnp.float32) * 0.02, 'gate_up_proj': jax.random.normal(k3, (NUM_EXPERTS, 2 * INTER, HIDDEN), dtype=jnp.float32) * 0.02, 'down_proj': jax.random.normal(k4, (NUM_EXPERTS, HIDDEN, INTER), dtype=jnp.float32) * 0.02, 'layer_alpha': jnp.array(1.0, dtype=jnp.float32)}
    _L0_ffn_all = _L0_ffn_setup()
    _L0_ffn_in = {k: v for k, v in _L0_ffn_all.items() if k in ('gate_weight', 'gate_up_proj', 'down_proj', 'layer_alpha')}
    del _L0_ffn_all
    return {'x': x, 'ctx_512': ctx_512, 'L0_attn_Wq': _L0_attn_in['Wq'], 'L0_attn_Wk': _L0_attn_in['Wk'], 'L0_attn_Wv': _L0_attn_in['Wv'], 'L0_attn_Wg': _L0_attn_in['Wg'], 'L0_attn_Wp': _L0_attn_in['Wp'], 'L0_xattn_Wq': _L0_xattn_in['Wq'], 'L0_xattn_w_kc_q': _L0_xattn_in['w_kc_q'], 'L0_xattn_w_kc_kv': _L0_xattn_in['w_kc_kv'], 'L0_xattn_W_qr': _L0_xattn_in['W_qr'], 'L0_xattn_W_kr': _L0_xattn_in['W_kr'], 'L0_xattn_Wo': _L0_xattn_in['Wo'], 'L0_ffn_gate_weight': _L0_ffn_in['gate_weight'], 'L0_ffn_gate_up_proj': _L0_ffn_in['gate_up_proj'], 'L0_ffn_down_proj': _L0_ffn_in['down_proj'], 'L0_ffn_layer_alpha': _L0_ffn_in['layer_alpha']}

def reference(x, ctx_512, L0_attn_Wq, L0_attn_Wk, L0_attn_Wv, L0_attn_Wg, L0_attn_Wp, L0_xattn_Wq, L0_xattn_w_kc_q, L0_xattn_w_kc_kv, L0_xattn_W_qr, L0_xattn_W_kr, L0_xattn_Wo, L0_ffn_gate_weight, L0_ffn_gate_up_proj, L0_ffn_down_proj, L0_ffn_layer_alpha):
    import jax
    import jax.numpy as jnp

    def _L0_attn_ref(x, Wq, Wk, Wv, Wg, Wp):
        import jax, jax.numpy as jnp
        import numpy as np
        B, N, D, BS = (2, 512, 256, 32)

        def rms_norm(x):
            eps = jnp.asarray(jnp.finfo(x.dtype).eps, x.dtype)
            return x * jax.lax.rsqrt(jnp.mean(x * x, axis=-1, keepdims=True) + eps)

        def la_kernel(q, k, v, bs):
            b, n, d = q.shape
            T = n // bs
            qc = q.reshape(b, T, bs, d).transpose(1, 0, 2, 3)
            kc = k.reshape(b, T, bs, d).transpose(1, 0, 2, 3)
            vc = v.reshape(b, T, bs, d).transpose(1, 0, 2, 3)
            mask = jnp.tril(jnp.ones((bs, bs), q.dtype))

            def step(kv, qkv):
                qt, kt, vt = qkv
                s = jnp.einsum('bid,bjd->bij', qt, kt) * mask
                ot = jnp.einsum('bij,bjd->bid', s, vt) + jnp.einsum('bid,bde->bie', qt, kv)
                kv = kv + jnp.einsum('bjd,bje->bde', kt, vt)
                return (kv, ot)
            kv0 = jnp.zeros((b, d, d), q.dtype)
            _, o = jax.lax.scan(step, kv0, (qc, kc, vc))
            return o.transpose(1, 0, 2, 3).reshape(b, n, d)
        xn = rms_norm(x)
        q = jax.nn.silu(jnp.einsum('bnd,od->bno', xn, Wq))
        k = jax.nn.silu(jnp.einsum('bnd,od->bno', xn, Wk))
        v = jax.nn.silu(jnp.einsum('bnd,od->bno', xn, Wv))
        g = jax.nn.sigmoid(jnp.einsum('bnd,od->bno', xn, Wg))
        o = la_kernel(q, k, v, BS) * g
        return jnp.einsum('bnd,od->bno', o, Wp)

    def _L0_xattn_ref(hidden_q, kv_c, Wq, w_kc_q, w_kc_kv, W_qr, W_kr, Wo):
        import jax, jax.numpy as jnp
        import numpy as np
        B, S, L = (2, 128, 128)
        DIM_Q, H, K, D_C, D_CQ, R = (256, 16, 128, 64, 192, 64)

        def _rope_tables(length, dim):
            inv = 1.0 / 10000.0 ** (jnp.arange(0, dim, 2, dtype=jnp.float32) / dim)
            f = jnp.arange(length, dtype=jnp.float32)[:, None] * inv[None, :]
            sin = jnp.repeat(jnp.sin(f), 2, axis=-1)
            cos = jnp.repeat(jnp.cos(f), 2, axis=-1)
            return (sin, cos)

        def _rotate_half(x):
            half = x.shape[-1] // 2
            return jnp.concatenate([-x[..., half:], x[..., :half]], axis=-1)

        def _apply_rope(x, sin, cos):
            return x * cos + _rotate_half(x) * sin
        Bv, Sv, _ = hidden_q.shape
        _, Lv, _ = kv_c.shape
        q_hk = (hidden_q @ Wq.T).reshape(Bv, Sv, H, K)
        q_big = jnp.einsum('bshk,hkq->bshq', q_hk, w_kc_q)
        sin_q, cos_q = _rope_tables(Sv, D_CQ)
        q_big = _apply_rope(q_big, sin_q[None, :, None, :], cos_q[None, :, None, :])
        sin_k, cos_k = _rope_tables(Lv, D_C)
        kv_r = _apply_rope(kv_c, sin_k[None], cos_k[None])
        q_r = jnp.einsum('bshq,hqr->bhsr', q_big, W_qr)
        k_r = jnp.einsum('bld,hdr->bhlr', kv_r, W_kr)
        scores = jnp.einsum('bhsr,bhlr->bhsl', q_r, k_r)
        attn = jax.nn.softmax(scores, axis=-1)
        ctx_c = jnp.einsum('bhsl,bld->bhsd', attn, kv_r)
        ctx_lat = jnp.einsum('bhsd,hkd->bhsk', ctx_c, w_kc_kv)
        ctx = ctx_lat.transpose(0, 2, 1, 3).reshape(Bv, Sv, H * K)
        return ctx @ Wo.T

    def _L0_ffn_ref(hidden_states, gate_weight, gate_up_proj, down_proj, layer_alpha):
        import jax
        import jax.numpy as jnp
        import numpy as np
        NUM_EXPERTS = 32
        HIDDEN = 256
        INTER = 96
        TOP_K = 8
        TAU = 0.05
        BATCH, SEQ = (2, 128)
        B, S, H = hidden_states.shape
        x = hidden_states.reshape(-1, H)
        T = x.shape[0]
        logits = x @ gate_weight.T
        probs = jax.nn.softmax(logits.astype(jnp.float32), axis=-1).astype(logits.dtype)
        topv, topi = jax.lax.top_k(probs, TOP_K)
        topv = topv / jnp.clip(topv.sum(axis=-1, keepdims=True), 1e-12)
        scaled = topv * layer_alpha.astype(topv.dtype)
        active = scaled >= TAU
        empty = ~jnp.any(active, axis=-1)
        fallback = jnp.arange(TOP_K)[None, :] == jnp.argmax(scaled, axis=-1)[:, None]
        active = active | empty[:, None] & fallback
        routing_weights = topv * active.astype(topv.dtype)
        routing_weights = routing_weights / jnp.clip(routing_weights.sum(axis=-1, keepdims=True), 1e-12)
        combine = jnp.zeros((T, NUM_EXPERTS), dtype=x.dtype)
        combine = combine.at[jnp.arange(T)[:, None], topi].add(routing_weights)

        def expert_step(acc, xs):
            w_gu, w_d, c_e = xs
            gu = x @ w_gu.T
            g, u = jnp.split(gu, 2, axis=-1)
            h = jax.nn.silu(g) * u
            acc = acc + h @ w_d.T * c_e[:, None]
            return (acc, None)
        out, _ = jax.lax.scan(expert_step, jnp.zeros_like(x), (gate_up_proj, down_proj, combine.T))
        return out.reshape(B, S, H)
    x = _layernorm(x + _L0_attn_ref(x, L0_attn_Wq, L0_attn_Wk, L0_attn_Wv, L0_attn_Wg, L0_attn_Wp), axis=-1)
    x = _layernorm(x + _L0_xattn_ref(x, ctx_512, L0_xattn_Wq, L0_xattn_w_kc_q, L0_xattn_w_kc_kv, L0_xattn_W_qr, L0_xattn_W_kr, L0_xattn_Wo), axis=-1)
    x = _layernorm(x + _L0_ffn_ref(x, L0_ffn_gate_weight, L0_ffn_gate_up_proj, L0_ffn_down_proj, L0_ffn_layer_alpha), axis=-1)
    return x

_drawn_inputs = setup_inputs


def setup_inputs(seed=0):
    import zlib

    import numpy as np

    out = dict(_drawn_inputs(seed))
    spreads = {}
    factors = {'L0_attn_Wg': 4.041,
     'L0_ffn_gate_weight': 8.0,
     'L0_ffn_gate_up_proj': 8.0,
     'L0_ffn_down_proj': 8.0}
    for name, (base, spread) in spreads.items():
        noise = np.random.default_rng([zlib.crc32(name.encode()), seed]).standard_normal(out[name].shape)
        drawn = base * np.exp(spread * noise) if base else spread * noise
        out[name] = jnp.asarray(drawn.astype(out[name].dtype))
    for name, factor in factors.items():
        out[name] = (out[name] * factor).astype(out[name].dtype)
    return out
```

```python
from contextlib import ExitStack

import numpy as np

import concourse.bass as bass
from concourse import mybir

F32 = mybir.dt.float32
F32R = mybir.dt.float32r
I32 = mybir.dt.int32
ALU = mybir.AluOpType
ACT = mybir.ActivationFunctionType
AX = mybir.AxisListType.X

P = 128
D = 256
KC = D // P
SEQ = 64
TOKENS = 32 * SEQ
TILES = 4
BT = TILES * P
BLOCKS = TOKENS // BT
SEQS = BT // SEQ
PAIRS = 8
DC = 64
DQ = 192
HALF = DQ // 2
EXPERTS = 32
INTER = 96
TOPK = 8
TAU = 0.05
GROUP = 4
ROWS = GROUP * INTER // P
SHARE = INTER // ROWS
GROUPS = EXPERTS // GROUP
GW = GROUP * INTER
LN_EPS = 1e-5
RMS_EPS = float(np.finfo(np.float32).eps)
RSQRT_SEED = 1597463007.0


def build(nc, a, out, c_dram):
    ctx = ExitStack()
    sb = lambda stack, name, shape, dt=F32: stack.enter_context(nc.sbuf_tensor(name, shape, dt))
    sem = lambda name: ctx.enter_context(nc.semaphore(name))

    x2T_all = sb(ctx, "x2T_all", [P, KC, TOKENS])
    c_all = sb(ctx, "c_all", [P, BLOCKS * TILES, EXPERTS])
    ident = sb(ctx, "ident", [P, P])

    att = ExitStack()
    w_hi = sb(att, "w_hi", [P, 4, KC, D], F32R)
    w_lo = sb(att, "w_lo", [P, 4, KC, D], F32R)
    a_hi = sb(att, "a_hi", [P, KC, PAIRS, 3 * P], F32R)
    a_lo = sb(att, "a_lo", [P, KC, PAIRS, 3 * P], F32R)
    m_w = sb(att, "m_w", [P, PAIRS, 3 * P])
    ropeq = sb(att, "ropeq", [P, 6, SEQ])
    ropek = sb(att, "ropek", [P, 2, DC])
    mask = sb(att, "mask", [P, P])
    wp = sb(att, "wp", [P, KC, D])
    xb = sb(att, "xb", [P, TILES, D])
    xn = sb(att, "xn", [P, TILES, D])
    xT_hi = sb(att, "xT_hi", [P, KC, BT], F32R)
    xT_lo = sb(att, "xT_lo", [P, KC, BT], F32R)
    st = sb(att, "st", [P, BT])
    qkgv = sb(att, "qkgv", [P, PAIRS, BT])
    lq = sb(att, "lq", [P, PAIRS, BT])
    u_w = sb(att, "u_w", [P, PAIRS, D])
    roped = sb(att, "roped", [P, 2, 3, BT])
    kv = sb(att, "kv", [P, SEQS, DC])
    kt = sb(att, "kt", [P, SEQS, DC])
    bd = sb(att, "bd", [P, SEQS, P])
    bdT = sb(att, "bdT", [P, SEQS, P])
    prod = sb(att, "prod", [P, 6, BT])
    x1 = sb(att, "x1", [P, TILES, D])
    x2T = sb(att, "x2T", [P, KC, BT])
    gate_w = sb(att, "gate_w", [P, KC, EXPERTS])
    rev_index = sb(att, "rev_index", [P, EXPERTS])
    alpha = sb(att, "alpha", [P, 1])
    small = sb(att, "small", [P, 160])
    stats = sb(att, "stats", [P, TILES, 6])
    rt = sb(att, "rt", [P, 4, TILES, EXPERTS])
    top = sb(att, "top", [P, TILES, TOPK])
    rs = sb(att, "rs", [P, 8, TILES])

    ss = small[:, 0:4]
    nt = small[:, 12:24].rearrange("p (k t) -> p k t", t=4)
    mv = small[:, 4:12].rearrange("p (t c) -> p t c", c=2)
    mx = small[:, 24:56].rearrange("p (k h) -> p k h", h=16)
    sm = small[:, 56:88].rearrange("p (k h) -> p k h", h=16)
    neg = small[:, 88:89]
    qT, kT, gT = qkgv[:, 0:2], qkgv[:, 2:4], qkgv[:, 4:6]
    v = qkgv[:, 6:8].rearrange("p a (t d) -> p (a t) d", d=D)
    e = prod[:, 0:4, :].rearrange("p (k a) n -> p k (a n)", k=2)
    flat = roped[:, :, :, :].rearrange("p a b n -> p (a b n)")
    at = flat[:, 0:2048].rearrange("p (k r s) -> p k r s", k=2, s=P)
    ct = flat[:, 2048:3072].rearrange("p (r s) -> p r s", s=P)
    raw_wq = lq[:, :, :].rearrange("p r n -> p (r n)").rearrange("p (h c) -> p h c", h=16)
    raw_kcq = flat.rearrange("p (h q) -> p h q", h=16)
    x2f = x2T_all[:, :, :].rearrange("p c n -> p (c n)")
    l_qr = x2f[:, 0:3072].rearrange("p (r t n) -> p r t n", r=PAIRS, t=3)
    r_kr = x2f[:, 3072:4096].rearrange("p (r n) -> p r n", r=PAIRS)
    raw_wo = x2f.rearrange("p (h n) -> p h n", h=16)
    raw_kv = prod[:, 0:2, :].rearrange("p a n -> p (a n)").rearrange("p (h d) -> p h d", h=16)
    raw_w = [prod[:, i, :].rearrange("p (c n) -> p c n", n=D) for i in range(2, 6)]
    att.close()

    ffn = ExitStack()
    f_raw = sb(ffn, "f_raw", [P, 2, KC * 2 * GW + ROWS * D])
    f_hi = sb(ffn, "f_hi", [P, 2, KC * 2 * GW + ROWS * D], F32R)
    f_lo = sb(ffn, "f_lo", [P, 2, KC * 2 * GW + ROWS * D], F32R)
    cT = sb(ffn, "cT", [P, TOKENS])
    cb = sb(ffn, "cb", [P, 2, TOKENS])
    y_hi = sb(ffn, "y_hi", [P, KC, TOKENS], F32R)
    y_lo = sb(ffn, "y_lo", [P, KC, TOKENS], F32R)
    sg = sb(ffn, "sg", [P, 2, BT])
    su = sb(ffn, "su", [P, 2, BT])
    hc = sb(ffn, "hc", [P, 2, BT])
    h_hi = sb(ffn, "h_hi", [P, 3, BT], F32R)
    h_lo = sb(ffn, "h_lo", [P, 3, BT], F32R)
    res = sb(ffn, "res", [P, BLOCKS, TILES, D])
    fst = sb(ffn, "fst", [P, TILES, 6])
    fsm = sb(ffn, "fsm", [P, 24])
    fmv = fsm[:, 0:8].rearrange("p (t c) -> p t c", c=2)
    fnt = fsm[:, 8:20].rearrange("p (k t) -> p k t", t=4)
    ffn.close()
    acc = x2T_all
    GU = KC * 2 * GW

    def gate_up(w, kc, gu, j):
        o = (kc * 2 + gu) * GW + j * P
        return w[:, o:o + P]

    def down(w, j, m):
        o = GU + j * D + m * P
        return w[:, o:o + P]

    ps = ctx.enter_context(nc.psum_tensor("ps", [P, 8, 512], F32))
    bank = lambda i: ps[:, i, :]

    s_ident, s_tables = sem("ident_loaded"), sem("tables_loaded")
    s_const, s_raw0, s_raw1, s_raw2, s_raw3 = map(sem, ("const_loaded", "raw_w_loaded", "raw_a_loaded", "raw_m_loaded", "raw_u_loaded"))
    s_whi, s_wlo = sem("w_hi_ready"), sem("w_lo_ready")
    s_zero = sem("zeros_ready")
    s_aps, s_ahi, s_alo = sem("a_in_psum"), sem("a_hi_ready"), sem("a_lo_ready")
    s_mps, s_m = sem("m_in_psum"), sem("m_ready")
    s_ups, s_u = sem("u_in_psum"), sem("u_ready")
    s_xb, s_xbfree = sem("x_loaded"), sem("x_buffer_free")
    s_kv, s_kvfree = sem("kv_loaded"), sem("kv_buffer_free")
    s_ss = sem("square_sums_ready")
    s_xn = sem("xn_ready")
    s_xt = sem("xT_in_psum")
    s_xthi, s_xtlo = sem("xT_hi_ready"), sem("xT_lo_ready")
    s_pj = sem("projection_in_psum")
    s_pa = sem("projection_ready")
    s_st, s_sm = sem("scores_in_psum"), sem("masked_scores_ready")
    s_ot, s_og = sem("context_in_psum"), sem("gated_context_ready")
    s_y, s_x1 = sem("attn_out_in_psum"), sem("x1_ready")
    s_bd, s_bdt, s_bdT = sem("kv_diagonal_ready"), sem("kvT_in_psum"), sem("kvT_ready")
    s_r1 = sem("attn_residual_ready")
    s_x1c = sem("x1_copied")
    s_th = sem("tanh_ready")
    s_x1t, s_x1hi, s_x1lo = sem("x1T_in_psum"), sem("x1T_hi_ready"), sem("x1T_lo_ready")
    s_q, s_rp, s_rope = sem("q_big_in_psum"), sem("rope_products_ready"), sem("roped_ready")
    s_qr, s_lq = sem("latent_q_in_psum"), sem("latent_q_ready")
    s_sc, s_sub, s_exp, s_nrm = sem("xscores_in_psum"), sem("shifted_ready"), sem("exp_ready"), sem("weights_ready")
    s_tp, s_at = sem("weightsT_in_psum"), sem("weightsT_ready")
    s_av, s_ct = sem("latent_ctx_in_psum"), sem("latent_ctx_ready")
    s_uo, s_r2, s_x2 = sem("xattn_out_in_psum"), sem("xattn_residual_ready"), sem("x2_ready")
    s_x2t, s_x2T = sem("x2T_in_psum"), sem("x2T_ready")
    s_lg = sem("logits_in_psum")
    s_lsub, s_lexp, s_c = sem("logits_shifted"), sem("logits_exp_ready"), sem("routing_ready")
    s_kept = sem("block_results_kept")
    s_own_v, s_kprod = sem("vector_own_steps"), sem("kv_products_ready")
    s_seqfree = sem("kv_diagonal_free")
    s_fload = [sem("even_expert_weights_loaded"), sem("odd_expert_weights_loaded")]
    s_fhi, s_flo = sem("expert_weights_hi"), sem("expert_weights_lo")
    s_ctp, s_cT, s_cdram = sem("cT_in_psum"), sem("cT_ready"), sem("cT_stored")
    s_cb = [[sem(f"routing_rows_{w}_{n}_loaded") for n in range(BLOCKS)] for w in range(2)]
    s_yhi, s_ylo = sem("y_hi_ready"), sem("y_lo_ready")
    s_g, s_up = sem("gate_in_psum"), sem("up_in_psum")
    s_sg, s_su, s_hc = sem("silu_ready"), sem("silu_up_ready"), sem("hidden_ready")
    s_hhi, s_hlo = sem("hidden_hi_ready"), sem("hidden_lo_ready")
    s_d, s_acc = sem("down_step_done"), sem("accumulated")
    s_ft, s_res, s_out = sem("ffn_out_in_psum"), sem("result_ready"), sem("result_stored")

    class Own:

        def __init__(self, eng, s):
            self.eng, self.s, self.n = eng, s, 0

        def step(self, ins):
            ins.then_inc(self.s, 1)
            self.n += 1
            return self.n

        def need(self, n=None):
            self.eng.wait_ge(self.s, self.n if n is None else n)

        def restart(self):
            self.need()
            self.eng.sem_clear(self.s)
            self.n = 0

    def split_matmuls(pe, dst, l_hi, l_lo, r_hi, r_lo, first, last, check=False):
        pe.matmul(dst, l_hi, r_hi, start=first, stop=False, skip_group_check=check)
        pe.matmul(dst, l_hi, r_lo, start=False, stop=False, skip_group_check=check)
        return pe.matmul(dst, l_lo, r_hi, start=False, stop=last, skip_group_check=check)

    def rsqrt(dve, own, value, y, t):
        own.need()
        own.step(dve.tensor_scalar(y.bitcast(I32), value.bitcast(I32), -0.5, RSQRT_SEED, ALU.mult, ALU.add))
        for _ in range(4):
            own.need()
            own.step(dve.tensor_tensor(t, y, y, ALU.mult))
            own.need()
            own.step(dve.scalar_tensor_tensor(out=t, in0=t, scalar=-0.5, in1=value, op0=ALU.mult, op1=ALU.mult))
            own.need()
            own.step(dve.scalar_tensor_tensor(out=y, in0=t, scalar=1.5, in1=y, op0=ALU.add, op1=ALU.mult))

    STEPS = 2 * BLOCKS * ROWS
    NB = 2 * BLOCKS

    def place(k):
        return k // (BLOCKS * ROWS) % 2, k // ROWS % BLOCKS, k % ROWS

    cols = lambda n: slice(n * BT, (n + 1) * BT)

    def over_groups(eng, body):
        body(0, True, False)
        with eng.Fori(0, GROUPS // 2 - 2) as i:
            body(i + 1, False, False)
        body(GROUPS // 2 - 1, False, True)

    def turn_c(pe, n):
        if n == LAST:
            pe.wait_ge(s_c, BLOCKS)
            pe.wait_ge(s_r2, 4 * BLOCKS)
        else:
            pe.wait_ge(s_kept, 32 * LAST + 1)
            if n >= 2:
                pe.wait_ge(s_cT, n - 1)
        for t in range(TILES):
            src = rt[:, 3, t, :] if n == LAST else c_all[:, TILES * n + t, :]
            mm = pe.transpose(ps[0:EXPERTS, (6, 7, 6, 4)[n], t * P:(t + 1) * P], src, ident[:])
        mm.then_inc(s_ctp, 1)

    def cT_out(act, n):
        act.wait_ge(s_q, 24 * BLOCKS)
        act.wait_ge(s_ctp, n + 1)
        act.activation(cT[0:EXPERTS, cols(n)], ps[0:EXPERTS, (6, 7, 6, 4)[n], :], ACT.Copy).then_inc(s_cT, 1)

    def y_hi_out(act, n):
        src = x2T[:] if n == LAST else x2T_all[:, :, cols(n)]
        if n == LAST:
            act.wait_ge(s_x2T, 4 * BLOCKS)
        else:
            act.wait_ge(s_q, 24 * BLOCKS)
            act.wait_ge(s_kept, 32 * LAST + 1)
        act.activation(y_hi[:, :, cols(n)], src, ACT.Copy).then_inc(s_yhi, 1)

    def y_lo_out(pool, n):
        src = x2T[:] if n == LAST else x2T_all[:, :, cols(n)]
        pool.wait_ge(s_yhi, n + 1)
        pool.tensor_tensor(y_lo[:, :, cols(n)], src, y_hi[:, :, cols(n)].bitcast(F32), ALU.subtract).then_inc(s_ylo, 1)

    def f_hi_out(act, w, part):
        s = slice(part * 768, (part + 1) * 768)
        act.activation(f_hi[:, w, s], f_raw[:, w, s], ACT.Copy).then_inc(s_fhi, 1)

    def f_lo_out(pool, w, g):
        pool.wait_ge(s_fhi, g * 3 + 3)
        pool.tensor_tensor(f_lo[:, w], f_raw[:, w], f_hi[:, w].bitcast(F32), ALU.subtract).then_inc(s_flo, 1)

    TURN_C = 7

    def ffn_scalar(act):
        act.wait_ge(s_lsub, BLOCKS)
        act.activation(rt[:, 1], rt[:, 0], ACT.Exp).then_inc(s_lexp, 1)

        def body(it, first, last):
            base = it * STEPS

            def hi(k):
                act.wait_ge(s_hc, base + k + 1)
                if not first or k >= 3:
                    act.wait_ge(s_d, base + k - 2)
                act.activation(h_hi[:, k % 3], hc[:, k % 2], ACT.Copy).then_inc(s_hhi, 1)

            for k in range(STEPS):
                act.wait_ge(s_g, base + k + 1)
                if not first or k >= 2:
                    act.wait_ge(s_su, base + k - 1)
                act.activation(sg[:, k % 2], bank(2 * (k % 2)), ACT.Silu).then_inc(s_sg, 1)
                if not first or k >= 1:
                    hi(k - 1)
                if first and k == 1:
                    y_hi_out(act, LAST)
                if first and k == TURN_C:
                    cT_out(act, LAST)
                if 4 <= k < 7:
                    if k == 4:
                        act.wait_ge(s_fload[1], it * 32 + 32)
                    f_hi_out(act, 1, k - 4)
                if 14 <= k < 17 and not last:
                    if k == 14:
                        act.wait_ge(s_fload[0], it * 32 + 64)
                        act.wait_ge(s_d, base + STEPS // 2)
                    f_hi_out(act, 0, k - 14)
            if last:
                hi(STEPS - 1)

        over_groups(act, body)

    def ffn_pool(pool):
        y_lo_out(pool, LAST)

        def body(it, first, last):
            f_lo_out(pool, 1, 2 * it + 1)
            if not last:
                f_lo_out(pool, 0, 2 * it + 2)

        over_groups(pool, body)

    def ffn_sync(sp, keep):
        def load(w, g):
            sp.dma_start(f_raw[:, w, 0:GU], a["L0_ffn_gate_up_proj"][g]).then_inc(s_fload[w], 16)
            sp.dma_start(f_raw[:, w, GU:], a["L0_ffn_down_proj"][g]).then_inc(s_fload[w], 16)

        def load_c(w, g, n):
            rows = c_dram[g, :, cols(n)].unsqueeze(1).broadcast_to((GROUP, SHARE, BT))
            sp.dma_start(cb[:, w, cols(n)], rows).then_inc(s_cb[w][n], 16)

        def store_c(n):
            sp.wait_ge(s_cT, n + 1)
            sp.dma_start(c_dram.rearrange("g e t -> (g e) t")[:, cols(n)], cT[0:EXPERTS, cols(n)]).then_inc(s_cdram, 16)
            sp.wait_ge(s_cdram, 16 * n + 16)
            load_c(0, 0, n)
            load_c(1, 1, n)

        sp.wait_ge(s_qr, PAIRS * BLOCKS)
        sp.wait_ge(s_q, 24 * BLOCKS)
        sp.wait_ge(s_kept, 32 * LAST + 1)
        load(0, 0)
        load(1, 1)
        for n in range(LAST):
            store_c(n)
        keep(LAST)
        store_c(LAST)
        with sp.Fori(0, GROUPS // 2 - 1) as it:
            for w in range(2):
                sp.wait_ge(s_flo, 2 * it + w + 1)
                load(w, 2 * it + w + 2)
            for w in range(2):
                for n in range(BLOCKS):
                    sp.wait_ge(s_hc, it * STEPS + w * (STEPS // 2) + ROWS * (n + 1))
                    load_c(w, 2 * it + w + 2, n)
        for n in range(BLOCKS):
            sp.wait_ge(s_res, TILES * (n + 1))
            sp.dma_start(out[n], res[:, n]).then_inc(s_out, 16)
        sp.wait_ge(s_out, 16 * BLOCKS)

    FINAL_BANKS = (4, 4, 4, 0)

    def ffn_vector(dve, own, route):
        dve.sem_inc(s_acc, 1)

        def final_norm(n, part):
            f = FINAL_BANKS[n]
            y = ps[:, f:f + 2, :].rearrange("p k (t d) -> p (k t) d", d=D)
            own.need()
            if part == 0:
                dve.wait_ge(s_ft, n + 1)
                for t in range(TILES):
                    own.step(dve.bn_stats(fst[:, t, :], y[:, t]))
            elif part == 1:
                for t in range(TILES):
                    own.step(dve.bn_aggr(fmv[:, t, :], fst[:, t, :]))
                own.need()
                own.step(dve.tensor_scalar(fnt[:, 0], fmv[:, :, 1], LN_EPS, None, ALU.add))
                rsqrt(dve, own, fnt[:, 0], fnt[:, 1], fnt[:, 2])
            else:
                for t in range(TILES):
                    dve.tensor_scalar(res[:, n, t], y[:, t], fmv[:, t, 0:1], fnt[:, 1, t:t + 1], ALU.subtract, ALU.mult)\
                        .then_inc(s_res, 1)
                dve.wait_ge(s_res, TILES * (n + 1))

        def body(it, first, last):
            base = it * STEPS

            def lo(k):
                dve.wait_ge(s_hhi, base + k + 1)
                if not first or k >= 3:
                    dve.wait_ge(s_d, base + k - 2)
                dve.tensor_tensor(h_lo[:, k % 3], hc[:, k % 2], h_hi[:, k % 3].bitcast(F32), ALU.subtract)\
                    .then_inc(s_hlo, 1)

            def accumulate(nb):
                n = nb % BLOCKS
                if first and nb == LAST:
                    dve.wait_ge(s_kept, 32 * LAST + 17)
                dve.wait_ge(s_d, base + ROWS * (nb + 1))
                dve.wait_ge(s_acc, it * NB + nb + 1)
                dve.tensor_tensor(acc[:, :, cols(n)], acc[:, :, cols(n)], ps[:, 6:8, :], ALU.add).then_inc(s_acc, 1)

            for k in range(STEPS):
                if (k - 5) % ROWS == 0 and (not first or k >= 5):
                    accumulate((k - 5) // ROWS)
                w, n, j = place(k)
                dve.wait_ge(s_sg, base + k + 1)
                dve.wait_ge(s_up, base + k + 1)
                dve.tensor_tensor(su[:, k % 2], sg[:, k % 2], bank(2 * (k % 2) + 1), ALU.mult).then_inc(s_su, 1)
                if j == 0:
                    dve.wait_ge(s_cb[w][n], it * 16 + 16)
                dve.wait_ge(s_su, base + k + 1)
                dve.tensor_tensor(hc[:, k % 2], su[:, k % 2], cb[:, w, cols(n)], ALU.mult).then_inc(s_hc, 1)
                if not first or k >= 1:
                    lo(k - 1)
                if first and k < 3:
                    route(LAST, k)
                if last and 19 <= k:
                    final_norm((k - 19) // 3, (k - 19) % 3)
            if last:
                lo(STEPS - 1)
                final_norm(1, 2)
                accumulate(NB - 1)
                for n in (2, 3):
                    for part in range(3):
                        final_norm(n, part)

        over_groups(dve, body)

    def ffn_tensor(pe):
        def body(it, first, last):
            base = it * STEPS

            def up(k):
                w, n, j = place(k)
                f = 2 * (k % 2)
                if k % (STEPS // 2) == 0:
                    pe.wait_ge(s_fhi, 3 * (2 * it + w) + 3)
                    pe.wait_ge(s_flo, 2 * it + w + 1)
                if first and j == 0 and k < BLOCKS * ROWS:
                    pe.wait_ge(s_ylo, n + 1)
                if first and k == 1:
                    pe.wait_ge(s_lsub, BLOCKS)
                if not first or k >= 2:
                    pe.wait_ge(s_su, base + k - 1)
                for gu, s in ((0, s_g), (1, s_up)):
                    for kc in range(KC):
                        mm = split_matmuls(pe, bank(f + gu), gate_up(f_hi[:, w], kc, gu, j), gate_up(f_lo[:, w], kc, gu, j),
                                           y_hi[:, kc, cols(n)], y_lo[:, kc, cols(n)], kc == 0, kc == KC - 1)
                    mm.then_inc(s, 1)

            def dn(k):
                w, n, j = place(k)
                pe.wait_ge(s_hlo, base + k + 1)
                if first and k == 0:
                    pe.wait_ge(s_cT, LAST)
                if j == 0:
                    pe.wait_ge(s_acc, it * NB + k // ROWS + 1)
                for m in range(KC):
                    mm = split_matmuls(pe, bank(6 + m), down(f_hi[:, w], j, m), down(f_lo[:, w], j, m),
                                       h_hi[:, k % 3], h_lo[:, k % 3], j == 0, j == ROWS - 1)
                mm.then_inc(s_d, 1)

            def turn_out(n):
                pe.wait_ge(s_acc, GROUPS * BLOCKS - BLOCKS + n + 2)
                if 1 <= n < LAST:
                    pe.wait_ge(s_res, TILES * n)
                f = FINAL_BANKS[n]
                for t in range(TILES):
                    for m in range(KC):
                        c = n * BT + t * P
                        mm = pe.transpose(ps[:, f + t // 2, (t % 2) * D + m * P:(t % 2) * D + (m + 1) * P],
                                          acc[:, m, c:c + P], ident[:])
                mm.then_inc(s_ft, 1)

            for k in range(STEPS):
                up(k)
                if not first or k >= 2:
                    dn(k - 2)
                if first and k == TURN_C:
                    turn_c(pe, LAST)
                if last and k == 18:
                    turn_out(0)
                if last and k == 21:
                    turn_out(1)
            if last:
                dn(STEPS - 2)
                dn(STEPS - 1)
                turn_out(2)
                pe.wait_ge(s_su, base + STEPS)
                turn_out(3)

        over_groups(pe, body)

    block = ctx.enter_context(nc.Block())
    LAST = BLOCKS - 1

    def over_blocks(eng, linear, pairs, cross):
        linear(0)
        pairs(0, False)
        with eng.Fori(0, LAST) as b:
            cross(b, True)
            pairs(b + 1, True)
        cross(LAST, False)

    @block.sync
    def _(sp):
        def load_x(b):
            sp.dma_start(xb[:], a["x"][b]).then_inc(s_xb, 16)

        def load_kv(b):
            for h in range(2):
                sp.dma_start(kv[64 * h:64 * h + 64, :, :], a["ctx_512"][b]).then_inc(s_kv, 16)

        load_x(0)
        sp.dma_start(ident[:], a["ident"]).then_inc(s_ident, 16)
        for i, name in enumerate(("L0_attn_Wq", "L0_attn_Wk", "L0_attn_Wv", "L0_attn_Wg")):
            sp.dma_start(raw_w[i], a[name]).then_inc(s_raw0, 16)
        qr, kr = a["L0_xattn_W_qr"], a["L0_xattn_W_kr"]
        sp.wait_ge(s_zero, 1)
        for dst, src in (
            (l_qr[0:64, :, 0, 0:96], qr[:, :, 0, 0:96]), (l_qr[0:64, :, 1, 0:96], qr[:, :, 0, 96:192]),
            (l_qr[64:128, :, 0, 96:128], qr[:, :, 1, 0:32]), (l_qr[64:128, :, 1, 96:128], qr[:, :, 1, 96:128]),
            (l_qr[64:128, :, 2, 0:64], qr[:, :, 1, 32:96]), (l_qr[64:128, :, 2, 64:128], qr[:, :, 1, 128:192]),
            (r_kr[0:64, :, 0:64], kr[:, :, 0, :]), (r_kr[64:128, :, 64:128], kr[:, :, 1, :]),
        ):
            sp.dma_start(dst, src).then_inc(s_raw2, 16)
        for dst, name in ((mask[:], "mask"), (ropek[:], "ropek"), (wp[:], "L0_attn_Wp")):
            sp.dma_start(dst, a[name]).then_inc(s_const, 16)
        load_kv(0)
        sp.dma_start(raw_kcq, a["L0_xattn_w_kc_q"]).then_inc(s_raw1, 16)
        sp.dma_start(raw_wq, a["L0_xattn_Wq"]).then_inc(s_raw1, 16)
        sp.wait_ge(s_wlo, 4)
        sp.dma_start(raw_kv, a["L0_xattn_w_kc_kv"]).then_inc(s_raw3, 16)
        for dst, name in ((ropeq[:], "ropeq"), (rev_index[:], "rev_index"), (gate_w[:], "L0_ffn_gate_weight")):
            sp.dma_start(dst, a[name]).then_inc(s_tables, 16)
        sp.dma_start(alpha[:], a["L0_ffn_layer_alpha"].broadcast_to((P, 1))).then_inc(s_tables, 16)
        sp.wait_ge(s_mps, PAIRS)
        sp.dma_start(raw_wo, a["L0_xattn_Wo"]).then_inc(s_raw3, 16)

        def keep(b):
            sp.wait_ge(s_x2T, 4 * b + 4)
            sp.dma_start(x2T_all[:, :, bass.ts(b, BT)], x2T[:]).then_inc(s_kept, 16)
            if b is LAST:
                return
            sp.wait_ge(s_c, b + 1)
            sp.dma_start(c_all[:, bass.ts(b, TILES), :], rt[:, 3, :, :]).then_inc(s_kept, 16)

        with sp.Fori(0, LAST) as b:
            sp.wait_ge(s_r1, 2 * b + 2)
            load_x(b + 1)
            sp.wait_ge(s_bd, 2 * b + 2)
            load_kv(b + 1)
            keep(b)
        ffn_sync(sp, keep)

    @block.gpsimd
    def _(pool):
        pool.memset(x2f, 0.0).then_inc(s_zero, 1)
        pool.memset(bd[:, :, :], 0.0).then_inc(s_zero, 1)
        pool.wait_ge(s_const, 3 * 16)
        pool.wait_ge(s_zero, 2)
        cosk = ropek[:, 0, :].unsqueeze(1).broadcast_to((P, SEQS, DC))

        def rope_kv(b):
            pool.wait_ge(s_kv, 32 * b + 32)
            for lo, src in ((0, 32), (32, 0)):
                sink = ropek[:, 1, lo:lo + 32].unsqueeze(1).broadcast_to((P, SEQS, 32))
                pool.tensor_tensor(kt[:, :, lo:lo + 32], kv[:, :, src:src + 32], sink, ALU.mult).then_inc(s_kprod, 1)
            pool.wait_ge(s_kprod, 3 * b + 2)
            pool.tensor_tensor(kv[:], kv[:], cosk, ALU.mult).then_inc(s_kprod, 1)

        def diagonal(b):
            pool.wait_ge(s_kprod, 3 * b + 3)
            for h in range(2):
                r = slice(64 * h, 64 * h + 64)
                if h:
                    pool.wait_ge(s_bd, 2 * b + 1)
                pool.tensor_tensor(bd[r, :, 64 * h:64 * h + 64], kv[r], kt[r], ALU.add).then_inc(s_bd, 1)
            pool.wait_ge(s_bd, 2 * b + 2)

        def linear(b):
            rope_kv(b)
            diagonal(b)

        def pairs(b, later):
            if later:
                pool.wait_ge(s_uo, 4 * b)
            for p in range(PAIRS):
                for k in range(3):
                    pool.wait_ge(s_rp, 24 * b + 3 * p + k + 1)
                    if p >= 2 and k == 0:
                        pool.wait_ge(s_qr, 8 * b + p - 1)
                    pool.tensor_tensor(roped[:, p % 2, k], prod[:, 2 * k], prod[:, 2 * k + 1], ALU.add)\
                        .then_inc(s_rope, 1)

        def cross(b, following):
            if following:
                rope_kv(b + 1)
                pool.wait_ge(s_seqfree, b + 1)
                diagonal(b + 1)
            else:
                for n in range(LAST):
                    y_lo_out(pool, n)
                    if n == 0:
                        f_lo_out(pool, 0, 0)

        over_blocks(pool, linear, pairs, cross)
        ffn_pool(pool)

    @block.scalar
    def _(act):
        def squares(b):
            act.wait_ge(s_xb, 16 * b + 16)
            for t in range(TILES):
                act.activation(xn[:, t], xb[:, t], ACT.Square, accum_out=ss[:, t:t + 1]).then_inc(s_ss, 1)

        def xT_hi_out(b, m, s_in, s_done):
            act.wait_ge(s_in, 2 * b + m + 1)
            act.activation(xT_hi[:, m], bank((6, 7)[m]), ACT.Copy).then_inc(s_done, 1)

        def tanh(b, i):
            act.wait_ge(s_pj, 8 * b + i + 1)
            act.activation(qkgv[:, (0, 1, 2, 3, 6, 7, 4, 5)[i]], bank(6 + i % 2), ACT.Tanh, scale=0.5).then_inc(s_th, 1)

        def bdT_out(b, i):
            act.wait_ge(s_bdt, 2 * b + i + 1)
            act.activation(bdT[:, 4 * i:4 * i + 4, :].rearrange("p s n -> p (s n)"), bank(6 + i), ACT.Copy)\
                .then_inc(s_bdT, 1)

        def a_hi_out(k):
            p, kc = k // KC, k % KC
            act.wait_ge(s_aps, k + 1)
            act.activation(a_hi[:, kc, p, :], ps[:, k % 4, 0:384], ACT.Copy).then_inc(s_ahi, 1)

        def linear(b):
            squares(b)
            act.wait_ge(s_raw0, 64)
            for i in range(4):
                act.activation(w_hi[:, i], raw_w[i], ACT.Copy).then_inc(s_whi, 1)
            xT_hi_out(b, 0, s_xt, s_xthi)
            xT_hi_out(b, 1, s_xt, s_xthi)
            tanh(b, 0)
            tanh(b, 1)
            for p in range(PAIRS):
                act.wait_ge(s_mps, p + 1)
                act.activation(m_w[:, p, :], ps[:, 4 + p % 2, 0:384], ACT.Copy).then_inc(s_m, 1)
            for i in range(2, 8):
                tanh(b, i)
            for k in range(12):
                a_hi_out(k)
            for p in range(PAIRS):
                act.wait_ge(s_ups, p + 1)
                act.activation(u_w[:, p, :], ps[:, 4 + p % 2, 0:D], ACT.Copy).then_inc(s_u, 1)
            xT_hi_out(b, 0, s_x1t, s_x1hi)
            xT_hi_out(b, 1, s_x1t, s_x1hi)
            for k in range(12, 16):
                a_hi_out(k)
            bdT_out(b, 0)
            bdT_out(b, 1)

        def pairs(b, later):
            act.wait_ge(s_x1, 4 * b + 4)
            if later:
                act.wait_ge(s_x2t, 4 * b)
            act.activation(x1[:], xn[:], ACT.Copy).then_inc(s_x1c, 1)
            if later:
                act.wait_ge(s_lsub, b)
                act.activation(rt[:, 1], rt[:, 0], ACT.Exp).then_inc(s_lexp, 1)
            for p in range(PAIRS):
                act.wait_ge(s_qr, 8 * b + p + 1)
                act.activation(lq[:, p], bank(6 + p % 2), ACT.Copy).then_inc(s_lq, 1)

        def cross(b, following):
            n = b + 1

            def expo(t):
                act.wait_ge(s_sub, 4 * b + t + 1)
                act.activation(e[:, t % 2], e[:, t % 2], ACT.Exp).then_inc(s_exp, 1)

            def turned(t):
                act.wait_ge(s_tp, 4 * b + t + 1)
                act.activation(at[:, t % 2], ps[:, 2:4, :].rearrange("p k (r s) -> p (k r) s", s=P), ACT.Copy)\
                    .then_inc(s_at, 1)

            def context(t):
                for h in range(2):
                    act.wait_ge(s_av, 8 * b + 2 * t + h + 1)
                    act.activation(ct[:, :, 64 * h:64 * h + 64], bank(4 + h).rearrange("p (r s) -> p r s", s=SEQ),
                                   ACT.Copy).then_inc(s_ct, 1)

            def x2T_out(t):
                act.wait_ge(s_x2t, 4 * b + t + 1)
                if t == 0:
                    act.wait_ge(s_kept, 32 * b + 1)
                act.activation(x2T[:, :, t * P:(t + 1) * P],
                               ps[:, 5, 0:KC * P].rearrange("p (c s) -> p c s", c=KC), ACT.Copy).then_inc(s_x2T, 1)

            if following:
                act.wait_ge(s_x1c, n)
                squares(n)
                xT_hi_out(n, 0, s_xt, s_xthi)
                xT_hi_out(n, 1, s_xt, s_xthi)
            expo(0)
            if following:
                tanh(n, 0)
                tanh(n, 1)
            expo(1)
            turned(0)
            if following:
                tanh(n, 2)
            context(0)
            if not following:
                cT_out(act, 0)
                cT_out(act, 1)
                y_hi_out(act, 0)
                act.wait_ge(s_fload[0], 32)
                f_hi_out(act, 0, 0)
            if following:
                tanh(n, 3)
                tanh(n, 4)
                tanh(n, 5)
            expo(2)
            turned(1)
            x2T_out(0)
            if following:
                tanh(n, 6)
            context(1)
            if following:
                tanh(n, 7)
            else:
                cT_out(act, 2)
                f_hi_out(act, 0, 1)
            turned(2)
            x2T_out(1)
            if not following:
                f_hi_out(act, 0, 2)
            expo(3)
            context(2)
            if not following:
                y_hi_out(act, 1)
            turned(3)
            x2T_out(2)
            context(3)
            if not following:
                y_hi_out(act, 2)
            if following:
                xT_hi_out(n, 0, s_x1t, s_x1hi)
                xT_hi_out(n, 1, s_x1t, s_x1hi)
            x2T_out(3)
            if following:
                bdT_out(n, 0)
                bdT_out(n, 1)

        over_blocks(act, linear, pairs, cross)
        ffn_scalar(act)

    @block.vector
    def _(dve):
        own = Own(dve, s_own_v)
        bc = lambda x, n: x.unsqueeze(2).broadcast_to((P, x.shape[1], n))

        def norm_rows(src, t0, n, s_done):
            for t in range(t0, t0 + n):
                own.step(dve.bn_stats(stats[:, t, :], src[:, t]))
            own.need()
            for t in range(t0, t0 + n):
                own.step(dve.bn_aggr(mv[:, t, :], stats[:, t, :]))
            own.need()
            val, y, w = (nt[:, k, t0:t0 + n] for k in range(3))
            own.step(dve.tensor_scalar(val, mv[:, t0:t0 + n, 1], LN_EPS, None, ALU.add))
            rsqrt(dve, own, val, y, w)
            own.need()
            for t in range(t0, t0 + n):
                dve.tensor_scalar(src[:, t], src[:, t], mv[:, t, 0:1], nt[:, 1, t:t + 1], ALU.subtract, ALU.mult)\
                    .then_inc(s_done, 1)

        def rms(b):
            dve.wait_ge(s_ss, 4 * b + 4)
            own.need()
            own.step(dve.tensor_scalar(nt[:, 0], ss, 1.0 / D, RMS_EPS, ALU.mult, ALU.add))
            rsqrt(dve, own, nt[:, 0], nt[:, 1], nt[:, 2])
            own.need()
            for t in range(TILES):
                dve.tensor_scalar(xn[:, t], xb[:, t], nt[:, 1, t:t + 1], None, ALU.mult).then_inc(s_xn, 1)

        def xT_lo_out(b, m, s_in, s_done):
            dve.wait_ge(s_in, 2 * b + m + 1)
            dve.tensor_tensor(xT_lo[:, m], bank(6 + m), xT_hi[:, m].bitcast(F32), ALU.subtract).then_inc(s_done, 1)

        def silu(b, i):
            dve.wait_ge(s_th, 8 * b + i + 1)
            dst = qkgv[:, (0, 1, 2, 3, 6, 7)[i]]
            dve.scalar_tensor_tensor(out=dst, in0=dst, scalar=1.0, in1=bank(6 + i % 2), op0=ALU.add, op1=ALU.mult)\
                .then_inc(s_pa, 1)

        def masked(b):
            dve.wait_ge(s_st, b + 1)
            dve.tensor_tensor(st[:].rearrange("p (t n) -> p t n", n=P), bank(6).rearrange("p (t n) -> p t n", n=P),
                              mask[:].unsqueeze(1).broadcast_to((P, TILES, P)), ALU.mult).then_inc(s_sm, 1)

        def gated(b, m):
            dve.wait_ge(s_ot, 2 * b + m + 1)
            dve.scalar_tensor_tensor(out=gT[:, m], in0=gT[:, m], scalar=1.0, in1=bank((7, 6)[m]),
                                     op0=ALU.add, op1=ALU.mult).then_inc(s_og, 1)

        def residual1(b, i):
            dve.wait_ge(s_y, 2 * b + i + 1)
            dve.scalar_tensor_tensor(
                out=xn[:, 2 * i:2 * i + 2], in0=bank(7 - i).rearrange("p (t n) -> p t n", n=D), scalar=1.0 / 16,
                in1=xb[:, 2 * i:2 * i + 2], op0=ALU.mult, op1=ALU.add).then_inc(s_r1, 1)

        def norm1(b):
            dve.wait_ge(s_r1, 2 * b + 2)
            own.need()
            norm_rows(xn, 0, TILES, s_x1)

        def a_lo_out(k):
            p, kc = k // KC, k % KC
            dve.wait_ge(s_ahi, k + 1)
            dve.tensor_tensor(a_lo[:, kc, p, :], ps[:, k % 4, 0:384], a_hi[:, kc, p, :].bitcast(F32), ALU.subtract)\
                .then_inc(s_alo, 1)

        def linear(b):
            rms(b)
            dve.wait_ge(s_raw0, 64)
            for i in range(4):
                dve.wait_ge(s_whi, i + 1)
                dve.tensor_tensor(w_lo[:, i], raw_w[i], w_hi[:, i].bitcast(F32), ALU.subtract).then_inc(s_wlo, 1)
            xT_lo_out(b, 0, s_xthi, s_xtlo)
            xT_lo_out(b, 1, s_xthi, s_xtlo)
            for i in range(6):
                silu(b, i)
            for k in range(4):
                a_lo_out(k)
            dve.wait_ge(s_const, 3 * 16)
            masked(b)
            for k in range(4, 8):
                a_lo_out(k)
            gated(b, 0)
            gated(b, 1)
            for k in range(8, 12):
                a_lo_out(k)
            residual1(b, 0)
            residual1(b, 1)
            norm1(b)
            xT_lo_out(b, 0, s_x1hi, s_x1lo)
            xT_lo_out(b, 1, s_x1hi, s_x1lo)
            for k in range(12, 16):
                a_lo_out(k)
            dve.wait_ge(s_tables, 4 * 16)
            own.step(dve.tensor_scalar(neg, alpha[:], 0.0, None, ALU.is_lt))
            own.restart()

        t64 = lambda ap: ap.rearrange("p (s n) -> p s n", n=SEQ)

        def times(dst, src, table, r=slice(0, P), o=slice(0, P)):
            return dve.tensor_tensor(
                t64(prod[o, dst, :]), t64(ps[r, src, :]),
                ropeq[r, table, :].unsqueeze(1).broadcast_to((r.stop - r.start, SEQS, SEQ)), ALU.mult)

        def pairs(b, later):
            own.need()
            for p in range(PAIRS):
                f = 3 * (p % 2)
                for k in range(3):
                    if p >= 1:
                        dve.wait_ge(s_rope, 24 * b + 3 * p - 2 + k)
                    if k < 2:
                        dve.wait_ge(s_q, 24 * b + 3 * p + 2)
                        times(2 * k, f + k, 2 * k)
                        times(2 * k + 1, f + 1 - k, 2 * k + 1).then_inc(s_rp, 1)
                    else:
                        dve.wait_ge(s_q, 24 * b + 3 * p + 3)
                        times(4, f + 2, 4)
                        times(5, f + 2, 5, slice(64, 128), slice(0, 64))
                        times(5, f + 2, 5, slice(0, 64), slice(64, 128)).then_inc(s_rp, 1)
                if later and p < 3:
                    route(b - 1, p)
            if later:
                own.restart()

        heads = lambda ap: ap.rearrange("p (h l) -> p h l", l=SEQ)

        def shift(b, t):
            dve.wait_ge(s_sc, 4 * b + t + 1)
            if t == 0:
                dve.wait_ge(s_rope, 24 * b + 24)
            if t >= 2:
                dve.wait_ge(s_tp, 4 * b + t - 1)
            sc = ps[:, 0:2, :].rearrange("p k (h l) -> p (k h) l", l=SEQ)
            own.need()
            own.step(dve.tensor_reduce(mx[:, t % 2], sc, AX, ALU.max))
            own.need()
            dve.tensor_tensor(heads(e[:, t % 2]), sc, bc(mx[:, t % 2], SEQ), ALU.subtract).then_inc(s_sub, 1)

        def normalise(b, t):
            dve.wait_ge(s_exp, 4 * b + t + 1)
            own.need()
            own.step(dve.tensor_reduce(sm[:, 0], heads(e[:, t % 2]), AX, ALU.add))
            own.need()
            own.step(dve.reciprocal(sm[:, 1], sm[:, 0]))
            own.need()
            dve.tensor_tensor(heads(e[:, t % 2]), heads(e[:, t % 2]), bc(sm[:, 1], SEQ), ALU.mult).then_inc(s_nrm, 1)

        def residual2(b, t):
            dve.wait_ge(s_uo, 4 * b + t + 1)
            if t == 0:
                dve.wait_ge(s_x1c, b + 1)
            dve.tensor_tensor(x1[:, t], ps[:, 4, 0:D], x1[:, t], ALU.add).then_inc(s_r2, 1)
            dve.wait_ge(s_r2, 4 * b + t + 1)
            own.need()
            norm_rows(x1, t, 1, s_x2)

        r0, r1, r2, r3 = (rt[:, k] for k in range(4))
        row = lambda k: rs[:, k, :]
        rb = lambda k: bc(row(k), EXPERTS)

        def tt(o, x, y, op):
            own.need()
            own.step(dve.tensor_tensor(o, x, y, op))

        def red(o, x, op):
            own.need()
            own.step(dve.tensor_reduce(o, x, AX, op))

        def shift_logits(b):
            lg = ps[:, 3, 0:TILES * EXPERTS].rearrange("p (t x) -> p t x", x=EXPERTS)
            dve.wait_ge(s_lg, b + 1)
            red(row(0), lg, ALU.max)
            own.need()
            dve.tensor_tensor(r0, lg, rb(0), ALU.subtract).then_inc(s_lsub, 1)

        def route(b, part):
            if part == 0:
                dve.wait_ge(s_lexp, b + 1)
                red(row(1), r1, ALU.add)
                own.need()
                own.step(dve.reciprocal(row(2), row(1)))
                tt(r0, r1, rb(2), ALU.mult)
                own.need()
                for t in range(TILES):
                    own.step(dve.max(top[:, t, :], r0[:, t]))
                own.need()
                for t in range(TILES):
                    own.step(dve.match_replace(r1[:, t], top[:, t, :], r0[:, t], -1.0))
                own.need()
                own.step(dve.scalar_tensor_tensor(out=r2, in0=r1, scalar=0.0, in1=r0, op0=ALU.is_lt, op1=ALU.mult))
            elif part == 1:
                red(row(0), r2, ALU.add)
                own.step(dve.tensor_tensor(row(3), top[:, :, 7], neg.broadcast_to((P, TILES)), ALU.mult))
                own.step(dve.tensor_scalar(rs[:, 4, 0:1], neg, -1.0, 1.0, ALU.mult, ALU.add))
                own.need()
                own.step(dve.tensor_scalar(row(1), row(0), 1e-12, None, ALU.max))
                own.step(dve.scalar_tensor_tensor(out=row(3), in0=top[:, :, 0], scalar=rs[:, 4, 0:1], in1=row(3),
                                                  op0=ALU.mult, op1=ALU.add))
                own.need()
                own.step(dve.reciprocal(row(2), row(1)))
                own.step(dve.tensor_tensor(r1, r0, rb(3), ALU.is_equal))
                own.need()
                own.step(dve.tensor_tensor(r2, r2, rb(2), ALU.mult))
                own.step(dve.tensor_tensor(r1, r1, rev_index[:].unsqueeze(1).broadcast_to((P, TILES, EXPERTS)),
                                           ALU.mult))
                red(row(5), r1, ALU.max)
                own.step(dve.tensor_scalar(r0, r2, alpha[:, 0:1], None, ALU.mult))
                tt(r1, r1, rb(5), ALU.is_equal)
                tt(r1, r1, r2, ALU.mult)
            else:
                red(row(6), r0, ALU.max)
                own.need()
                own.step(dve.tensor_scalar(row(7), row(6), TAU, None, ALU.is_lt))
                own.step(dve.scalar_tensor_tensor(out=r2, in0=r0, scalar=TAU, in1=r2, op0=ALU.is_ge, op1=ALU.mult))
                tt(r1, r1, rb(7), ALU.mult)
                tt(r2, r2, r1, ALU.add)
                red(row(0), r2, ALU.add)
                own.need()
                own.step(dve.tensor_scalar(row(1), row(0), 1e-12, None, ALU.max))
                own.need()
                own.step(dve.reciprocal(row(2), row(1)))
                own.need()
                dve.wait_ge(s_kept, 32 * b + 1)
                dve.tensor_tensor(r3, r2, rb(2), ALU.mult).then_inc(s_c, 1)

        def cross(b, following):
            n = b + 1
            if following:
                rms(n)
            shift(b, 0)
            if following:
                xT_lo_out(n, 0, s_xthi, s_xtlo)
                xT_lo_out(n, 1, s_xthi, s_xtlo)
            normalise(b, 0)
            shift(b, 1)
            if following:
                silu(n, 0)
                silu(n, 1)
            normalise(b, 1)
            if following:
                silu(n, 2)
                silu(n, 3)
            residual2(b, 0)
            shift(b, 2)
            if following:
                silu(n, 4)
                silu(n, 5)
            normalise(b, 2)
            residual2(b, 1)
            shift(b, 3)
            if following:
                masked(n)
            normalise(b, 3)
            if following:
                gated(n, 0)
                gated(n, 1)
            residual2(b, 2)
            if following:
                residual1(n, 0)
                residual1(n, 1)
                norm1(n)
            residual2(b, 3)
            if following:
                xT_lo_out(n, 0, s_x1hi, s_x1lo)
                xT_lo_out(n, 1, s_x1hi, s_x1lo)
            shift_logits(b)

        over_blocks(dve, linear, pairs, cross)
        ffn_vector(dve, own, route)

    @block.tensor
    def _(pe):
        def turn_x(b, m, s_in, s_done):
            for t in range(TILES):
                pe.wait_ge(s_in, 4 * b + t + 1)
                mm = pe.transpose(ps[:, 6 + m, t * P:(t + 1) * P], xn[:, t, m * P:(m + 1) * P], ident[:])
            mm.then_inc(s_done, 1)

        def projection(b, i):
            w, m = (0, 1, 2, 3)[i // 2], i % 2
            if i == 0:
                pe.wait_ge(s_xtlo, 2 * b + 2)
            if i >= 2:
                pe.wait_ge(s_pa, 6 * b + i - 1)
            if w == 2:
                for t in (2 * m, 2 * m + 1):
                    s = slice(t * P, (t + 1) * P)
                    for kc in range(KC):
                        mm = split_matmuls(pe, ps[:, 6 + m, (t % 2) * D:(t % 2 + 1) * D], xT_hi[:, kc, s],
                                           xT_lo[:, kc, s], w_hi[:, w, kc, :], w_lo[:, w, kc, :],
                                           kc == 0, kc == KC - 1)
            else:
                s = slice(m * P, (m + 1) * P)
                for kc in range(KC):
                    mm = split_matmuls(pe, bank(6 + m), w_hi[:, w, kc, s], w_lo[:, w, kc, s], xT_hi[:, kc, :],
                                       xT_lo[:, kc, :], kc == 0, kc == KC - 1)
            mm.then_inc(s_pj, 1)

        def self_scores(b):
            pe.wait_ge(s_th, 8 * b + 7)
            for t in range(TILES):
                s = slice(t * P, (t + 1) * P)
                for kc in range(KC):
                    mm = pe.matmul(ps[:, 6, s], kT[:, kc, s], qT[:, kc, s], start=kc == 0, stop=kc == KC - 1)
            mm.then_inc(s_st, 1)

        def self_context(b, m):
            if m == 0:
                pe.wait_ge(s_th, 8 * b + 8)
                pe.wait_ge(s_pa, 6 * b + 6)
                pe.wait_ge(s_sm, b + 1)
            for t in range(TILES):
                s = slice(t * P, (t + 1) * P)
                mm = pe.matmul(ps[:, 7 - m, s], v[:, t, m * P:(m + 1) * P], st[:, s], start=True, stop=True)
            mm.then_inc(s_ot, 1)

        def attn_out(b, i):
            pe.wait_ge(s_og, 2 * b + 2)
            for t in (2 * i, 2 * i + 1):
                for kc in range(KC):
                    mm = pe.matmul(ps[:, 7 - i, (t % 2) * D:(t % 2 + 1) * D], gT[:, kc, t * P:(t + 1) * P],
                                   wp[:, kc, :], start=kc == 0, stop=kc == KC - 1)
            mm.then_inc(s_y, 1)

        def turn_kv(b, i):
            pe.wait_ge(s_bd, 2 * b + 2)
            pe.wait_ge(s_x1lo, 2 * b + i + 1)
            for q in range(4 * i, 4 * i + 4):
                mm = pe.transpose(ps[:, 6 + i, (q % 4) * P:(q % 4 + 1) * P], bd[:, q, :], ident[:])
            mm.then_inc(s_bdt, 1)

        def fold_m():
            pe.wait_ge(s_raw2, 8 * 16)
            for p in range(PAIRS):
                if p >= 2:
                    pe.wait_ge(s_m, p - 1)
                for t in range(3):
                    mm = pe.matmul(ps[:, 4 + p % 2, t * P:(t + 1) * P], l_qr[:, p, t, :], r_kr[:, p, :],
                                   start=True, stop=True)
                mm.then_inc(s_mps, 1)

        def fold_a(k0, k1):
            pe.wait_ge(s_raw1, 32)
            for k in range(k0, k1):
                p, kc = k // KC, k % KC
                if k >= 4:
                    pe.wait_ge(s_alo, k - 3)
                o = ps[:, k % 4, 0:384]
                l = [raw_wq[:, 2 * p + h, kc * P:(kc + 1) * P] for h in range(2)]
                w0 = raw_kcq[:, 2 * p, :].rearrange("p (g q) -> p g q", g=2)
                w1 = raw_kcq[:, 2 * p + 1, :].rearrange("p (g q) -> p g q", g=2)
                ab = o[:, 0:256].rearrange("p (g q) -> p g q", g=2)
                pe.matmul(ab[:, :, 0:96], l[0], w0, start=True, stop=True)
                pe.matmul(ab[:, :, 96:128], l[1], w1[:, :, 0:32], start=True, stop=True)
                pe.matmul(o[:, 256:384].rearrange("p (g q) -> p g q", g=2), l[1], w1[:, :, 32:96],
                          start=True, stop=True).then_inc(s_aps, 1)

        def fold_u():
            pe.wait_ge(s_raw3, 32)
            pe.wait_ge(s_m, PAIRS)
            for p in range(PAIRS):
                if p >= 2:
                    pe.wait_ge(s_u, p - 1)
                for h in range(2):
                    mm = pe.matmul(ps[64 * h:64 * h + 64, 4 + p % 2, 0:D], raw_kv[:, 2 * p + h, :],
                                   raw_wo[:, 2 * p + h, :], start=True, stop=True)
                mm.then_inc(s_ups, 1)

        def linear(b):
            pe.wait_ge(s_ident, 16)
            turn_x(b, 0, s_xn, s_xt)
            turn_x(b, 1, s_xn, s_xt)
            pe.wait_ge(s_wlo, 4)
            projection(b, 0)
            projection(b, 1)
            fold_m()
            for i in range(2, 8):
                projection(b, i)
            fold_a(0, 4)
            self_scores(b)
            fold_a(4, 8)
            self_context(b, 0)
            self_context(b, 1)
            fold_a(8, 12)
            pe.wait_ge(s_const, 3 * 16)
            attn_out(b, 0)
            attn_out(b, 1)
            fold_u()
            turn_x(b, 0, s_x1, s_x1t)
            turn_x(b, 1, s_x1, s_x1t)
            fold_a(12, 16)
            turn_kv(b, 0)
            turn_kv(b, 1)
            pe.wait_ge(s_u, PAIRS)
            pe.wait_ge(s_alo, PAIRS * KC)
            pe.wait_ge(s_tables, 4 * 16)
            pe.sem_inc(s_kept, 1)

        def pairs(b, later):
            def latent_q(p):
                if p == 0:
                    pe.wait_ge(s_bdT, 2 * b + 2)
                if p >= 2:
                    pe.wait_ge(s_lq, 8 * b + p - 1)
                for k in range(3):
                    pe.wait_ge(s_rope, 24 * b + 3 * p + k + 1)
                    mm = pe.matmul(bank(6 + p % 2), m_w[:, p, k * P:(k + 1) * P], roped[:, p % 2, k, :],
                                   start=k == 0, stop=k == 2)
                mm.then_inc(s_qr, 1)

            pe.wait_ge(s_x1lo, 2 * b + 2)
            if later:
                pe.wait_ge(s_lsub, b)
            for p in range(PAIRS):
                if p >= 2:
                    pe.wait_ge(s_rp, 24 * b + 3 * p - 3)
                for k in range(3):
                    s = slice(k * P, (k + 1) * P)
                    for kc in range(KC):
                        mm = split_matmuls(pe, bank(3 * (p % 2) + k), a_hi[:, kc, p, s], a_lo[:, kc, p, s],
                                           xT_hi[:, kc, :], xT_lo[:, kc, :], kc == 0, kc == KC - 1)
                    mm.then_inc(s_q, 1)
                if p >= 1:
                    latent_q(p - 1)
            latent_q(PAIRS - 1)

        def cross(b, following):
            n = b + 1

            def scores(t):
                pe.wait_ge(s_rp, 24 * b + 24)
                if t >= 1:
                    pe.wait_ge(s_sub, 4 * b + t)
                for p in range(PAIRS):
                    if t == 0:
                        pe.wait_ge(s_lq, 8 * b + p + 1)
                    for h in range(2):
                        mm = pe.matmul(ps[64 * h:64 * h + 64, p // 4, (p % 4) * P:(p % 4 + 1) * P],
                                       lq[:, p, t * P + 64 * h:t * P + 64 * h + 64], bdT[:, 2 * t + h, :],
                                       start=True, stop=True)
                mm.then_inc(s_sc, 1)

            def turn(t):
                pe.wait_ge(s_nrm, 4 * b + t + 1)
                for p in range(PAIRS):
                    mm = pe.transpose(ps[:, 2 + p // 4, (p % 4) * P:(p % 4 + 1) * P], e[:, t % 2, p * P:(p + 1) * P],
                                      ident[:])
                mm.then_inc(s_tp, 1)

            def context(t):
                pe.wait_ge(s_at, 4 * b + t + 1)
                if t >= 1:
                    pe.wait_ge(s_r2, 4 * b + t)
                for h in range(2):
                    if t >= 1 and h == 1:
                        pe.wait_ge(s_x2T, 4 * b + t)
                    pe.matmul(bank(4 + h), bd[:, 2 * t + h, :], at[:, t % 2, :, 64 * h:64 * h + 64],
                              start=True, stop=True).then_inc(s_av, 1)

            def project(t):
                pe.wait_ge(s_ct, 8 * b + 2 * t + 2)
                for p in range(PAIRS):
                    mm = pe.matmul(ps[:, 4, 0:D], ct[:, p, :], u_w[:, p, :], start=p == 0, stop=p == PAIRS - 1)
                mm.then_inc(s_uo, 1)

            def turn_x2(t):
                pe.wait_ge(s_x2, 4 * b + t + 1)
                for m in range(KC):
                    mm = pe.transpose(ps[:, 5, m * P:(m + 1) * P], x1[:, t, m * P:(m + 1) * P], ident[:])
                mm.then_inc(s_x2t, 1)

            scores(0)
            if following:
                turn_x(n, 0, s_xn, s_xt)
                turn_x(n, 1, s_xn, s_xt)
            scores(1)
            if following:
                projection(n, 0)
                projection(n, 1)
            else:
                turn_c(pe, 0)
                turn_c(pe, 1)
            turn(0)
            if following:
                projection(n, 2)
            context(0)
            if following:
                projection(n, 3)
            project(0)
            scores(2)
            if following:
                projection(n, 4)
                projection(n, 5)
            turn(1)
            turn_x2(0)
            if following:
                projection(n, 6)
            context(1)
            if following:
                projection(n, 7)
            project(1)
            scores(3)
            if following:
                self_scores(n)
            else:
                turn_c(pe, 2)
            turn(2)
            turn_x2(1)
            if following:
                self_context(n, 0)
            context(2)
            if following:
                self_context(n, 1)
            project(2)
            if following:
                attn_out(n, 0)
            turn(3)
            turn_x2(2)
            if following:
                attn_out(n, 1)
            context(3)
            pe.drain().then_inc(s_seqfree, 1)
            project(3)
            if following:
                turn_x(n, 0, s_x1, s_x1t)
                turn_x(n, 1, s_x1, s_x1t)
            turn_x2(3)
            if following:
                turn_kv(n, 0)
                turn_kv(n, 1)
            pe.wait_ge(s_x2T, 4 * b + 4)
            pe.wait_ge(s_at, 4 * b + 4)
            for t in range(TILES):
                for kc in range(KC):
                    mm = pe.matmul(ps[:, 3, t * EXPERTS:(t + 1) * EXPERTS], x2T[:, kc, t * P:(t + 1) * P],
                                   gate_w[:, kc, :], start=kc == 0, stop=kc == KC - 1)
            mm.then_inc(s_lg, 1)

        over_blocks(pe, linear, pairs, cross)
        ffn_tensor(pe)

    ctx.close()


def _constants():
    f = np.float32
    c = {"ident": np.eye(P, dtype=f)}
    j, i = np.arange(P)[:, None], np.arange(P)[None, :]
    c["mask"] = ((j // SEQ == i // SEQ) & (j <= i)).astype(f)

    def table(dim):
        inv = (f(1.0) / np.power(f(10000.0), np.arange(0, dim, 2, dtype=f) / f(dim))).astype(f)
        ang = np.repeat(np.arange(SEQ, dtype=f)[:, None] * inv[None, :], 2, axis=1)
        return np.sin(ang).astype(f), np.cos(ang).astype(f)

    sin, cos = table(DQ)
    up = np.r_[0:96, 0:32]
    cu = np.r_[32:96]
    c["ropeq"] = np.ascontiguousarray(np.stack([
        cos[:, up].T, -sin[:, up].T, cos[:, up + HALF].T, sin[:, up + HALF].T,
        np.concatenate([cos[:, cu], cos[:, cu + HALF]], 1).T,
        np.concatenate([sin[:, cu + HALF], -sin[:, cu]], 1).T], axis=1)).astype(f)
    sin, cos = table(DC)
    sin = np.concatenate([-sin[:, :32], sin[:, 32:]], 1)
    c["ropek"] = np.ascontiguousarray(np.tile(np.stack([cos, sin], axis=1), (2, 1, 1))).astype(f)
    c["rev_index"] = np.tile(np.arange(EXPERTS, 0, -1, dtype=f)[None], (P, 1))
    return c


def kernel(**inputs):
    import concourse.bacc as bacc
    from concourse.bass_utils import run_bass_kernel_spmd as run

    x = {k: np.asarray(v) for k, v in inputs.items()}
    tiles = lambda w: w.reshape(-1, P, w.shape[-1]).transpose(1, 0, 2)
    lay = {
        "x": x["x"].reshape(BLOCKS, TILES, P, D).transpose(0, 2, 1, 3),
        "ctx_512": x["ctx_512"].reshape(BLOCKS, SEQS, SEQ, DC).transpose(0, 2, 1, 3),
        **{n: tiles(x[n].T) for n in ("L0_attn_Wq", "L0_attn_Wk", "L0_attn_Wv", "L0_attn_Wg", "L0_attn_Wp",
                                      "L0_ffn_gate_weight", "L0_xattn_Wo")},
        "L0_xattn_Wq": tiles(x["L0_xattn_Wq"]),
        "L0_xattn_w_kc_q": x["L0_xattn_w_kc_q"].transpose(1, 0, 2),
        "L0_xattn_w_kc_kv": x["L0_xattn_w_kc_kv"].transpose(1, 0, 2),
        "L0_xattn_W_qr": x["L0_xattn_W_qr"].reshape(PAIRS, 2, DQ, 64).transpose(3, 0, 1, 2),
        "L0_xattn_W_kr": x["L0_xattn_W_kr"].reshape(PAIRS, 2, DC, 64).transpose(3, 0, 1, 2),
        "L0_ffn_gate_up_proj": x["L0_ffn_gate_up_proj"].reshape(GROUPS, GROUP, 2, ROWS, SHARE, KC, P)
                               .transpose(0, 6, 5, 2, 3, 1, 4).reshape(GROUPS, P, KC * 2 * GW),
        "L0_ffn_down_proj": x["L0_ffn_down_proj"].transpose(0, 2, 1).reshape(GROUPS, GROUP, ROWS, SHARE, D)
                            .transpose(0, 1, 3, 2, 4).reshape(GROUPS, P, ROWS * D),
        "L0_ffn_layer_alpha": x["L0_ffn_layer_alpha"].reshape(1, 1),
        **_constants(),
    }
    nc = bacc.Bacc("TRN2", target_bir_lowering=False, num_devices=1)
    arrays = {n: np.ascontiguousarray(v) for n, v in lay.items()}
    aps = {n: nc.dram_tensor("in_" + n, v.shape, mybir.dt.from_np(v.dtype), kind="ExternalInput").ap()
           for n, v in arrays.items()}
    out = nc.dram_tensor("out", (BLOCKS, P, TILES, D), F32, kind="ExternalOutput").ap()
    c_dram = nc.dram_tensor("routing", (GROUPS, GROUP, TOKENS), F32).ap()
    build(nc, aps, out, c_dram)
    got = run(nc, [{"in_" + n: v for n, v in arrays.items()}], core_ids=[0]).results[0]["out"]
    return np.ascontiguousarray(got.transpose(0, 2, 1, 3)).reshape(32, SEQ, D)
```

```python
from contextlib import ExitStack

import numpy as np

import concourse.bass as bass
from concourse import mybir

F32 = mybir.dt.float32
F32R = mybir.dt.float32r
I32 = mybir.dt.int32
ALU = mybir.AluOpType
ACT = mybir.ActivationFunctionType
AX = mybir.AxisListType.X

P = 128
D = 256
KC = D // P
SEQ = 64
TOKENS = 32 * SEQ
TILES = 4
BT = TILES * P
BLOCKS = TOKENS // BT
SEQS = BT // SEQ
PAIRS = 8
DC = 64
DQ = 192
HALF = DQ // 2
EXPERTS = 32
INTER = 96
TOPK = 8
TAU = 0.05
GROUP = 4
ROWS = GROUP * INTER // P
SHARE = INTER // ROWS
GROUPS = EXPERTS // GROUP
GW = GROUP * INTER
LN_EPS = 1e-5
RMS_EPS = float(np.finfo(np.float32).eps)
RSQRT_SEED = 1597463007.0


def build(nc, a, out, c_dram):
    ctx = ExitStack()
    sb = lambda stack, name, shape, dt=F32: stack.enter_context(nc.sbuf_tensor(name, shape, dt))
    sem = lambda name: ctx.enter_context(nc.semaphore(name))

    x2T_all = sb(ctx, "x2T_all", [P, KC, TOKENS])
    c_all = sb(ctx, "c_all", [P, BLOCKS * TILES, EXPERTS])
    ident = sb(ctx, "ident", [P, P])

    att = ExitStack()
    w_hi = sb(att, "w_hi", [P, 4, KC, D], F32R)
    w_lo = sb(att, "w_lo", [P, 4, KC, D], F32R)
    a_hi = sb(att, "a_hi", [P, KC, PAIRS, 3 * P], F32R)
    a_lo = sb(att, "a_lo", [P, KC, PAIRS, 3 * P], F32R)
    m_w = sb(att, "m_w", [P, PAIRS, 3 * P])
    ropeq = sb(att, "ropeq", [P, 6, SEQ])
    ropek = sb(att, "ropek", [P, 2, DC])
    mask = sb(att, "mask", [P, P])
    wp = sb(att, "wp", [P, KC, D])
    xb = sb(att, "xb", [P, TILES, D])
    xn = sb(att, "xn", [P, TILES, D])
    xT_hi = sb(att, "xT_hi", [P, KC, BT], F32R)
    xT_lo = sb(att, "xT_lo", [P, KC, BT], F32R)
    st = sb(att, "st", [P, BT])
    qkgv = sb(att, "qkgv", [P, PAIRS, BT])
    lq = sb(att, "lq", [P, PAIRS, BT])
    u_w = sb(att, "u_w", [P, PAIRS, D])
    roped = sb(att, "roped", [P, 2, 3, BT])
    kv = sb(att, "kv", [P, SEQS, DC])
    kt = sb(att, "kt", [P, SEQS, DC])
    bd = sb(att, "bd", [P, SEQS, P])
    bdT = sb(att, "bdT", [P, SEQS, P])
    prod = sb(att, "prod", [P, 6, BT])
    x1 = sb(att, "x1", [P, TILES, D])
    x2T = sb(att, "x2T", [P, KC, BT])
    gate_w = sb(att, "gate_w", [P, KC, EXPERTS])
    rev_index = sb(att, "rev_index", [P, EXPERTS])
    alpha = sb(att, "alpha", [P, 1])
    small = sb(att, "small", [P, 160])
    stats = sb(att, "stats", [P, TILES, 6])
    rt = sb(att, "rt", [P, 4, TILES, EXPERTS])
    top = sb(att, "top", [P, TILES, TOPK])
    rs = sb(att, "rs", [P, 8, TILES])

    ss = small[:, 0:4]
    nt = small[:, 12:24].rearrange("p (k t) -> p k t", t=4)
    mv = small[:, 4:12].rearrange("p (t c) -> p t c", c=2)
    mx = small[:, 24:56].rearrange("p (k h) -> p k h", h=16)
    sm = small[:, 56:88].rearrange("p (k h) -> p k h", h=16)
    neg = small[:, 88:89]
    half = small[:, 89:90]
    qT, kT, gT = qkgv[:, 0:2], qkgv[:, 2:4], qkgv[:, 4:6]
    v = qkgv[:, 6:8].rearrange("p a (t d) -> p (a t) d", d=D)
    e = prod[:, 0:4, :].rearrange("p (k a) n -> p k (a n)", k=2)
    flat = roped[:, :, :, :].rearrange("p a b n -> p (a b n)")
    at = flat[:, 0:2048].rearrange("p (k r s) -> p k r s", k=2, s=P)
    ct = flat[:, 2048:3072].rearrange("p (r s) -> p r s", s=P)
    raw_wq = lq[:, :, :].rearrange("p r n -> p (r n)").rearrange("p (h c) -> p h c", h=16)
    raw_kcq = flat.rearrange("p (h q) -> p h q", h=16)
    x2f = x2T_all[:, :, :].rearrange("p c n -> p (c n)")
    l_qr = x2f[:, 0:3072].rearrange("p (r t n) -> p r t n", r=PAIRS, t=3)
    r_kr = x2f[:, 3072:4096].rearrange("p (r n) -> p r n", r=PAIRS)
    raw_wo = x2f.rearrange("p (h n) -> p h n", h=16)
    raw_kv = prod[:, 0:2, :].rearrange("p a n -> p (a n)").rearrange("p (h d) -> p h d", h=16)
    raw_w = [prod[:, i, :].rearrange("p (c n) -> p c n", n=D) for i in range(2, 6)]
    att.close()

    ffn = ExitStack()
    f_raw = sb(ffn, "f_raw", [P, 2, KC * 2 * GW + ROWS * D])
    f_hi = sb(ffn, "f_hi", [P, 2, KC * 2 * GW + ROWS * D], F32R)
    f_lo = sb(ffn, "f_lo", [P, 2, KC * 2 * GW + ROWS * D], F32R)
    cT = sb(ffn, "cT", [P, TOKENS])
    cb = sb(ffn, "cb", [P, 2, TOKENS])
    y_hi = sb(ffn, "y_hi", [P, KC, TOKENS], F32R)
    y_lo = sb(ffn, "y_lo", [P, KC, TOKENS], F32R)
    sg = sb(ffn, "sg", [P, 2, BT])
    su = sb(ffn, "su", [P, 2, BT])
    hc = sb(ffn, "hc", [P, 2, BT])
    h_hi = sb(ffn, "h_hi", [P, 3, BT], F32R)
    h_lo = sb(ffn, "h_lo", [P, 3, BT], F32R)
    res = sb(ffn, "res", [P, BLOCKS, TILES, D])
    fst = sb(ffn, "fst", [P, TILES, 6])
    fsm = sb(ffn, "fsm", [P, 24])
    fscale = sb(ffn, "fscale", [P, BLOCKS, 2, TILES])
    fmv = fsm[:, 0:8].rearrange("p (t c) -> p t c", c=2)
    fnt = fsm[:, 8:20].rearrange("p (k t) -> p k t", t=4)
    ffn.close()
    acc = x2T_all
    GU = KC * 2 * GW

    def gate_up(w, kc, gu, j):
        o = (kc * 2 + gu) * GW + j * P
        return w[:, o:o + P]

    def down(w, j, m):
        o = GU + j * D + m * P
        return w[:, o:o + P]

    ps = ctx.enter_context(nc.psum_tensor("ps", [P, 8, 512], F32))
    bank = lambda i: ps[:, i, :]
    KV_BANKS = (3, 5)
    LOGITS = ps[:, 7, KC * P:KC * P + TILES * EXPERTS]
    LAST_LOGITS = ps[:, 4, 0:TILES * EXPERTS]

    s_ident, s_tables = sem("ident_loaded"), sem("tables_loaded")
    s_raw0 = [sem(f"raw_w{c}_loaded") for c in "qkvg"]
    s_const, s_raw1, s_raw2, s_raw3 = map(sem, ("const_loaded", "raw_a_loaded", "raw_m_loaded", "raw_u_loaded"))
    s_whi, s_wlo = sem("w_hi_ready"), sem("w_lo_ready")
    s_zero = sem("zeros_ready")
    s_aps, s_ahi, s_alo = sem("a_in_psum"), sem("a_hi_ready"), sem("a_lo_ready")
    s_mps, s_m = sem("m_in_psum"), sem("m_ready")
    s_ups, s_u = sem("u_in_psum"), sem("u_ready")
    s_xb, s_kv = sem("x_loaded"), sem("kv_loaded")
    s_ss = sem("square_sums_ready")
    s_xn = sem("xn_ready")
    s_xt = sem("xT_in_psum")
    s_xthi, s_xtlo = sem("xT_hi_ready"), sem("xT_lo_ready")
    s_pj = sem("projection_in_psum")
    s_pa = sem("projection_ready")
    s_st, s_sm = sem("scores_in_psum"), sem("masked_scores_ready")
    s_ot, s_og = sem("context_in_psum"), sem("gated_context_ready")
    s_y, s_x1 = sem("attn_out_in_psum"), sem("x1_ready")
    s_bd, s_bdt, s_bdT = sem("kv_diagonal_ready"), sem("kvT_in_psum"), sem("kvT_ready")
    s_r1 = sem("attn_residual_ready")
    s_x1c = sem("x1_copied")
    s_th = sem("tanh_ready")
    s_x1t, s_x1hi, s_x1lo = sem("x1T_in_psum"), sem("x1T_hi_ready"), sem("x1T_lo_ready")
    s_q, s_rp, s_rope = sem("q_big_in_psum"), sem("rope_products_ready"), sem("roped_ready")
    s_qr, s_lq = sem("latent_q_in_psum"), sem("latent_q_ready")
    s_sc, s_sub, s_exp, s_nrm = sem("xscores_in_psum"), sem("shifted_ready"), sem("exp_ready"), sem("weights_ready")
    s_tp, s_at = sem("weightsT_in_psum"), sem("weightsT_ready")
    s_av, s_ct = sem("latent_ctx_in_psum"), sem("latent_ctx_ready")
    s_uo, s_r2, s_x2 = sem("xattn_out_in_psum"), sem("xattn_residual_ready"), sem("x2_ready")
    s_x2t, s_x2T = sem("x2T_in_psum"), sem("x2T_ready")
    s_lg = sem("logits_in_psum")
    s_lsub, s_lexp, s_c = sem("logits_shifted"), sem("logits_exp_ready"), sem("routing_ready")
    s_kept = sem("block_results_kept")
    s_own_v, s_kprod = sem("vector_own_steps"), sem("kv_products_ready")
    s_seqfree = sem("kv_diagonal_free")
    s_fload = [sem("even_expert_weights_loaded"), sem("odd_expert_weights_loaded")]
    s_fhi, s_flo = sem("expert_weights_hi"), sem("expert_weights_lo")
    s_ctp, s_cT, s_cdram = sem("cT_in_psum"), sem("cT_ready"), sem("cT_stored")
    s_cb = [[sem(f"routing_rows_{w}_{n}_loaded") for n in range(BLOCKS)] for w in range(2)]
    s_yhi, s_ylo = sem("y_hi_ready"), sem("y_lo_ready")
    s_g, s_up = sem("gate_in_psum"), sem("up_in_psum")
    s_sg, s_su, s_hc = sem("silu_ready"), sem("silu_up_ready"), sem("hidden_ready")
    s_hhi, s_hlo = sem("hidden_hi_ready"), sem("hidden_lo_ready")
    s_d, s_acc = sem("down_step_done"), sem("accumulated")
    s_res_end = sem("last_tiles_ready")
    s_ft, s_scale, s_res, s_out = sem("ffn_out_in_psum"), sem("final_scale_ready"), sem("result_ready"), sem("result_stored")

    class Own:

        def __init__(self, eng, s):
            self.eng, self.s, self.n = eng, s, 0

        def step(self, ins):
            ins.then_inc(self.s, 1)
            self.n += 1
            return self.n

        def need(self, n=None):
            self.eng.wait_ge(self.s, self.n if n is None else n)

        def restart(self):
            self.need()
            self.eng.sem_clear(self.s)
            self.n = 0

    def split_matmuls(pe, dst, l_hi, l_lo, r_hi, r_lo, first, last, check=False):
        pe.matmul(dst, l_hi, r_hi, start=first, stop=False, skip_group_check=check)
        pe.matmul(dst, l_hi, r_lo, start=False, stop=False, skip_group_check=check)
        return pe.matmul(dst, l_lo, r_hi, start=False, stop=last, skip_group_check=check)

    def rsqrt(dve, own, value, y, t, half=None):
        own.need()
        own.step(dve.tensor_scalar(y.bitcast(I32), value.bitcast(I32), -0.5, RSQRT_SEED, ALU.mult, ALU.add))
        for _ in range(3):
            own.need()
            if half is not None:
                own.step(dve.scalar_tensor_tensor(out=t, in0=y, scalar=half, in1=y, op0=ALU.mult, op1=ALU.mult))
            else:
                own.step(dve.tensor_tensor(t, y, y, ALU.mult))
                own.need()
                own.step(dve.scalar_tensor_tensor(out=t, in0=t, scalar=-0.5, in1=value, op0=ALU.mult, op1=ALU.mult))
            own.need()
            own.step(dve.scalar_tensor_tensor(out=y, in0=t, scalar=1.5, in1=y, op0=ALU.add, op1=ALU.mult))

    STEPS = 2 * BLOCKS * ROWS
    NB = 2 * BLOCKS

    def place(k):
        return k // (BLOCKS * ROWS) % 2, k // ROWS % BLOCKS, k % ROWS

    cols = lambda n: slice(n * BT, (n + 1) * BT)

    def over_groups(eng, body):
        body(0, True, False)
        with eng.Fori(0, GROUPS // 2 - 2) as i:
            body(i + 1, False, False)
        body(GROUPS // 2 - 1, False, True)

    C_BANKS = (6, 7, 5, 4)

    def turn_c(pe, n):
        if n == LAST:
            pe.wait_ge(s_c, BLOCKS)
        else:
            pe.wait_ge(s_kept, 32 * LAST + 1)
        for t in range(TILES):
            src = rt[:, 3, t, :] if n == LAST else c_all[:, TILES * n + t, :]
            mm = pe.transpose(ps[0:EXPERTS, C_BANKS[n], t * P:(t + 1) * P], src, ident[:])
        mm.then_inc(s_ctp, 1)

    def cT_out(act, n):
        act.wait_ge(s_q, 24 * BLOCKS)
        act.wait_ge(s_ctp, n + 1)
        act.activation(cT[0:EXPERTS, cols(n)], ps[0:EXPERTS, C_BANKS[n], :], ACT.Copy).then_inc(s_cT, 1)

    def y_hi_out(act, n):
        src = x2T[:] if n == LAST else x2T_all[:, :, cols(n)]
        if n == LAST:
            act.wait_ge(s_x2T, 4 * BLOCKS)
        else:
            act.wait_ge(s_q, 24 * BLOCKS)
            act.wait_ge(s_kept, 32 * LAST + 1)
        act.activation(y_hi[:, :, cols(n)], src, ACT.Copy).then_inc(s_yhi, 1)

    def y_lo_out(pool, n):
        src = x2T[:] if n == LAST else x2T_all[:, :, cols(n)]
        pool.wait_ge(s_yhi, n + 1)
        pool.tensor_tensor(y_lo[:, :, cols(n)], src, y_hi[:, :, cols(n)].bitcast(F32), ALU.subtract).then_inc(s_ylo, 1)

    def f_hi_out(act, w, part):
        s = slice(part * 768, (part + 1) * 768)
        act.activation(f_hi[:, w, s], f_raw[:, w, s], ACT.Copy).then_inc(s_fhi, 1)

    def f_lo_out(pool, w, g):
        pool.wait_ge(s_fhi, g * 3 + 3)
        pool.tensor_tensor(f_lo[:, w], f_raw[:, w], f_hi[:, w].bitcast(F32), ALU.subtract).then_inc(s_flo, 1)

    def h_lo_out(eng, done, k, used=True):
        eng.wait_ge(s_hhi, done + 1)
        if used:
            eng.wait_ge(s_d, done - 2)
        if eng is nc.gpsimd and k == POOL_STEP:
            eng.wait_ge(s_hlo, done)
        eng.tensor_tensor(h_lo[:, k % 3], hc[:, k % 2], h_hi[:, k % 3].bitcast(F32), ALU.subtract).then_inc(s_hlo, 1)

    TURN_C = 7

    X2_STEP, LOGITS_STEP, ROUTE_STEPS = 0, 1, (1, 2, 3, 4, 5, 6)

    FINAL_BANKS = (4, 4, 0, 2)
    POOL_STEP = 17
    FINAL_STEP = 18

    def final_sum(n):
        f = FINAL_BANKS[n]
        return ps[:, f:f + 2, :].rearrange("p k (t d) -> p (k t) d", d=D)

    def ffn_scalar(act, x2T_out):
        def body(it, first, last):
            base = it * STEPS

            def hi(k):
                act.wait_ge(s_hc, base + k + 1)
                if not first or k >= 3:
                    act.wait_ge(s_d, base + k - 2)
                act.activation(h_hi[:, k % 3], hc[:, k % 2], ACT.Copy).then_inc(s_hhi, 1)

            for k in range(STEPS):
                act.wait_ge(s_g, base + k + 1)
                if not first or k >= 2:
                    act.wait_ge(s_su, base + k - 1)
                act.activation(sg[:, k % 2], bank(2 * (k % 2)), ACT.Silu).then_inc(s_sg, 1)
                if not first or k >= 1:
                    hi(k - 1)
                if first and k == X2_STEP:
                    x2T_out(LAST, 2, 7)
                    x2T_out(LAST, 3, 5)
                if first and k == LOGITS_STEP:
                    act.wait_ge(s_lsub, BLOCKS)
                    act.activation(rt[:, 1], rt[:, 0], ACT.Exp).then_inc(s_lexp, 1)
                if first and k == 3:
                    y_hi_out(act, LAST)
                if first and k == TURN_C:
                    cT_out(act, LAST)
                if 4 <= k < 7:
                    if k == 4:
                        act.wait_ge(s_fload[1], it * 32 + 32)
                    f_hi_out(act, 1, k - 4)
                if 14 <= k < 17 and not last:
                    if k == 14:
                        act.wait_ge(s_fload[0], it * 32 + 64)
                        act.wait_ge(s_d, base + STEPS // 2)
                    f_hi_out(act, 0, k - 14)
                if last and k == FINAL_STEP + 3:
                    final_apply(0)
            if last:
                hi(STEPS - 1)
                final_apply(1)
                final_apply(2)
                final_apply(3)

        def final_apply(n):
            y = final_sum(n)
            act.wait_ge(s_scale, n + 1)
            for t in range(2 if n == LAST else TILES):
                act.activation(res[:, n, t], y[:, t], ACT.Identity, bias=fscale[:, n, 1, t:t + 1],
                               scale=fscale[:, n, 0, t:t + 1]).then_inc(s_res, 1)

        over_groups(act, body)

    def ffn_pool(pool):
        y_lo_out(pool, LAST)

        def body(it, first, last):
            f_lo_out(pool, 1, 2 * it + 1)
            if not last:
                f_lo_out(pool, 0, 2 * it + 2)
            else:
                for k in range(POOL_STEP, STEPS):
                    h_lo_out(pool, it * STEPS + k, k)

        over_groups(pool, body)

    def ffn_sync(sp, keep_x2):
        def load(w, g):
            sp.dma_start(f_raw[:, w, 0:GU], a["L0_ffn_gate_up_proj"][g]).then_inc(s_fload[w], 16)
            sp.dma_start(f_raw[:, w, GU:], a["L0_ffn_down_proj"][g]).then_inc(s_fload[w], 16)

        def load_c(w, g, n):
            rows = c_dram[g, :, cols(n)].unsqueeze(1).broadcast_to((GROUP, SHARE, BT))
            sp.dma_start(cb[:, w, cols(n)], rows).then_inc(s_cb[w][n], 16)

        def store_c(n):
            sp.wait_ge(s_cT, n + 1)
            sp.dma_start(c_dram.rearrange("g e t -> (g e) t")[:, cols(n)], cT[0:EXPERTS, cols(n)]).then_inc(s_cdram, 16)
            sp.wait_ge(s_cdram, 16 * n + 16)
            load_c(0, 0, n)
            load_c(1, 1, n)

        sp.wait_ge(s_qr, PAIRS * BLOCKS)
        sp.wait_ge(s_q, 24 * BLOCKS)
        sp.wait_ge(s_kept, 32 * LAST + 1)
        load(0, 0)
        load(1, 1)
        for n in range(LAST):
            store_c(n)
        keep_x2(LAST)
        store_c(LAST)
        with sp.Fori(0, GROUPS // 2 - 1) as it:
            for w in range(2):
                sp.wait_ge(s_flo, 2 * it + w + 1)
                load(w, 2 * it + w + 2)
            for w in range(2):
                for n in range(BLOCKS):
                    sp.wait_ge(s_hc, it * STEPS + w * (STEPS // 2) + ROWS * (n + 1))
                    load_c(w, 2 * it + w + 2, n)
        for n in range(BLOCKS):
            sp.wait_ge(s_res, TILES * (n + 1) - 2 * (n == LAST))
            if n == LAST:
                sp.wait_ge(s_res_end, 2)
            sp.dma_start(out[n], res[:, n]).then_inc(s_out, 16)
        sp.wait_ge(s_out, 16 * BLOCKS)

    def ffn_vector(dve, own, shift_logits, route):
        dve.sem_inc(s_acc, 1)

        def final_norm(n, part):
            y = final_sum(n)
            own.need()
            if part == 0:
                dve.wait_ge(s_ft, n + 1)
                for t in range(TILES):
                    own.step(dve.bn_stats(fst[:, t, :], y[:, t]))
            else:
                for t in range(TILES):
                    own.step(dve.bn_aggr(fmv[:, t, :], fst[:, t, :]))
                own.need()
                own.step(dve.tensor_scalar(fnt[:, 0], fmv[:, :, 1], LN_EPS, None, ALU.add))
                rsqrt(dve, own, fnt[:, 0], fscale[:, n, 0], fnt[:, 2])
                own.need()
                dve.scalar_tensor_tensor(out=fscale[:, n, 1], in0=fmv[:, :, 0], scalar=-1.0, in1=fscale[:, n, 0],
                                         op0=ALU.mult, op1=ALU.mult).then_inc(s_scale, 1)
                dve.wait_ge(s_scale, n + 1)

        def body(it, first, last):
            base = it * STEPS

            def lo(k):
                h_lo_out(dve, base + k, k, not first or k >= 3)

            def accumulate(nb):
                n = nb % BLOCKS
                if first and nb == LAST:
                    dve.wait_ge(s_kept, 32 * LAST + 17)
                dve.wait_ge(s_d, base + ROWS * (nb + 1))
                dve.wait_ge(s_acc, it * NB + nb + 1)
                dve.tensor_tensor(acc[:, :, cols(n)], acc[:, :, cols(n)], ps[:, 6:8, :], ALU.add).then_inc(s_acc, 1)

            for k in range(STEPS):
                if (k - 5) % ROWS == 0 and (not first or k >= 5):
                    accumulate((k - 5) // ROWS)
                w, n, j = place(k)
                dve.wait_ge(s_sg, base + k + 1)
                dve.wait_ge(s_up, base + k + 1)
                dve.tensor_tensor(su[:, k % 2], sg[:, k % 2], bank(2 * (k % 2) + 1), ALU.mult).then_inc(s_su, 1)
                if j == 0:
                    dve.wait_ge(s_cb[w][n], it * 16 + 16)
                if last and k >= POOL_STEP + 2:
                    dve.wait_ge(s_hlo, base + k - 1)
                dve.wait_ge(s_su, base + k + 1)
                dve.tensor_tensor(hc[:, k % 2], su[:, k % 2], cb[:, w, cols(n)], ALU.mult).then_inc(s_hc, 1)
                if (not first or k >= 1) and not (last and k > POOL_STEP):
                    lo(k - 1)
                if first and k == LOGITS_STEP:
                    shift_logits(LAST, LAST_LOGITS)
                if first and k in ROUTE_STEPS:
                    route(LAST, ROUTE_STEPS.index(k))
                if last and k in (FINAL_STEP + 1, FINAL_STEP + 2):
                    final_norm(0, k - FINAL_STEP - 1)
                if last and k == FINAL_STEP + 4:
                    final_norm(1, 0)
            if last:
                final_norm(1, 1)
                final_norm(2, 0)
                accumulate(NB - 1)
                final_norm(2, 1)
                final_norm(3, 0)
                final_norm(3, 1)
                y = final_sum(LAST)
                for t in (2, 3):
                    dve.tensor_scalar(res[:, LAST, t], y[:, t], fmv[:, t, 0:1], fscale[:, LAST, 0, t:t + 1],
                                      ALU.subtract, ALU.mult).then_inc(s_res_end, 1)

        over_groups(dve, body)

    def ffn_tensor(pe, turn_x2, logits):
        def body(it, first, last):
            base = it * STEPS

            def up(k):
                w, n, j = place(k)
                f = 2 * (k % 2)
                if k % (STEPS // 2) == 0:
                    pe.wait_ge(s_fhi, 3 * (2 * it + w) + 3)
                    pe.wait_ge(s_flo, 2 * it + w + 1)
                if first and j == 0 and k < BLOCKS * ROWS:
                    pe.wait_ge(s_ylo, n + 1)
                if first and k == 0:
                    pe.wait_ge(s_sub, 8 * BLOCKS)
                if first and k == 1:
                    pe.wait_ge(s_at, 4 * BLOCKS)
                if not first or k >= 2:
                    pe.wait_ge(s_su, base + k - 1)
                for gu, s in ((0, s_g), (1, s_up)):
                    for kc in range(KC):
                        mm = split_matmuls(pe, bank(f + gu), gate_up(f_hi[:, w], kc, gu, j), gate_up(f_lo[:, w], kc, gu, j),
                                           y_hi[:, kc, cols(n)], y_lo[:, kc, cols(n)], kc == 0, kc == KC - 1)
                    mm.then_inc(s, 1)

            def dn(k):
                w, n, j = place(k)
                pe.wait_ge(s_hlo, base + k + 1)
                if first and k == 0:
                    pe.wait_ge(s_r2, 4 * BLOCKS)
                    pe.wait_ge(s_x2T, 4 * BLOCKS)
                if j == 0:
                    pe.wait_ge(s_acc, it * NB + k // ROWS + 1)
                for m in range(KC):
                    mm = split_matmuls(pe, bank(6 + m), down(f_hi[:, w], j, m), down(f_lo[:, w], j, m),
                                       h_hi[:, k % 3], h_lo[:, k % 3], j == 0, j == ROWS - 1)
                mm.then_inc(s_d, 1)

            def turn_out(n):
                pe.wait_ge(s_acc, GROUPS * BLOCKS - BLOCKS + n + 2)
                if n == 1:
                    pe.wait_ge(s_res, TILES)
                if n >= 2:
                    pe.wait_ge(s_su, GROUPS * BLOCKS * ROWS + n - LAST)
                f = FINAL_BANKS[n]
                for t in range(TILES):
                    for m in range(KC):
                        c = n * BT + t * P
                        mm = pe.transpose(ps[:, f + t // 2, (t % 2) * D + m * P:(t % 2) * D + (m + 1) * P],
                                          acc[:, m, c:c + P], ident[:])
                mm.then_inc(s_ft, 1)

            for k in range(STEPS):
                up(k)
                if not first or k >= 2:
                    dn(k - 2)
                if first and k == X2_STEP:
                    pe.wait_ge(s_x2T, 4 * BLOCKS - 2)
                    turn_x2(LAST, 2, 7)
                    pe.wait_ge(s_ct, 8 * BLOCKS)
                    turn_x2(LAST, 3, 5)
                if first and k == LOGITS_STEP:
                    logits(LAST, LAST_LOGITS)
                if first and k == TURN_C:
                    turn_c(pe, LAST)
                if last and k == FINAL_STEP:
                    turn_out(0)
                if last and k == FINAL_STEP + 3:
                    turn_out(1)
            if last:
                dn(STEPS - 2)
                turn_out(2)
                dn(STEPS - 1)
                turn_out(3)

        over_groups(pe, body)

    block = ctx.enter_context(nc.Block())
    LAST = BLOCKS - 1

    def over_blocks(eng, linear, pairs, cross):
        linear(0)
        pairs(0, False, True)
        with eng.Fori(0, LAST - 1) as b:
            cross(b, True)
            pairs(b + 1, True, True)
        cross(LAST - 1, True)
        pairs(LAST, True, False)
        cross(LAST, False)

    @block.sync
    def _(sp):
        def load_x(b):
            sp.dma_start(xb[:], a["x"][b]).then_inc(s_xb, 16)

        def load_kv(b):
            for h in range(2):
                sp.dma_start(kv[64 * h:64 * h + 64, :, :], a["ctx_512"][b]).then_inc(s_kv, 16)

        load_x(0)
        sp.dma_start(ident[:], a["ident"]).then_inc(s_ident, 16)
        for i, name in enumerate(("L0_attn_Wq", "L0_attn_Wk", "L0_attn_Wv", "L0_attn_Wg")):
            sp.dma_start(raw_w[i], a[name]).then_inc(s_raw0[i], 16)
        qr, kr = a["L0_xattn_W_qr"], a["L0_xattn_W_kr"]
        sp.wait_ge(s_zero, 1)
        for dst, src in (
            (l_qr[0:64, :, 0, 0:96], qr[:, :, 0, 0:96]), (l_qr[0:64, :, 1, 0:96], qr[:, :, 0, 96:192]),
            (l_qr[64:128, :, 0, 96:128], qr[:, :, 1, 0:32]), (l_qr[64:128, :, 1, 96:128], qr[:, :, 1, 96:128]),
            (l_qr[64:128, :, 2, 0:64], qr[:, :, 1, 32:96]), (l_qr[64:128, :, 2, 64:128], qr[:, :, 1, 128:192]),
            (r_kr[0:64, :, 0:64], kr[:, :, 0, :]), (r_kr[64:128, :, 64:128], kr[:, :, 1, :]),
        ):
            sp.dma_start(dst, src).then_inc(s_raw2, 16)
        for dst, name in ((mask[:], "mask"), (ropek[:], "ropek"), (wp[:], "L0_attn_Wp")):
            sp.dma_start(dst, a[name]).then_inc(s_const, 16)
        load_kv(0)
        sp.dma_start(raw_kcq, a["L0_xattn_w_kc_q"]).then_inc(s_raw1, 16)
        sp.dma_start(raw_wq, a["L0_xattn_Wq"]).then_inc(s_raw1, 16)
        sp.wait_ge(s_wlo, 4)
        sp.dma_start(raw_kv, a["L0_xattn_w_kc_kv"]).then_inc(s_raw3, 16)
        for dst, name in ((ropeq[:], "ropeq"), (rev_index[:], "rev_index"), (gate_w[:], "L0_ffn_gate_weight")):
            sp.dma_start(dst, a[name]).then_inc(s_tables, 16)
        sp.dma_start(alpha[:], a["L0_ffn_layer_alpha"].broadcast_to((P, 1))).then_inc(s_tables, 16)
        sp.wait_ge(s_mps, PAIRS)
        sp.dma_start(raw_wo, a["L0_xattn_Wo"]).then_inc(s_raw3, 16)

        def keep_x2(b):
            sp.wait_ge(s_x2T, 4 * b + 4)
            sp.dma_start(x2T_all[:, :, bass.ts(b, BT)], x2T[:]).then_inc(s_kept, 16)

        def keep_c(b):
            sp.wait_ge(s_c, b + 1)
            sp.dma_start(c_all[:, bass.ts(b, TILES), :], rt[:, 3, :, :]).then_inc(s_kept, 16)

        def next_kv(b):
            sp.wait_ge(s_bd, 2 * b + 2)
            load_kv(b + 1)

        def next_x(b):
            sp.wait_ge(s_r1, 2 * b + 2)
            load_x(b + 1)

        next_x(0)
        with sp.Fori(0, LAST - 1) as b:
            next_kv(b)
            keep_x2(b)
            next_x(b + 1)
            keep_c(b)
        next_kv(LAST - 1)
        keep_x2(LAST - 1)
        keep_c(LAST - 1)
        ffn_sync(sp, keep_x2)

    @block.gpsimd
    def _(pool):
        pool.memset(x2f, 0.0).then_inc(s_zero, 1)
        pool.memset(bd[:, :, :], 0.0).then_inc(s_zero, 1)
        pool.wait_ge(s_const, 3 * 16)
        pool.wait_ge(s_zero, 2)
        cosk = ropek[:, 0, :].unsqueeze(1).broadcast_to((P, SEQS, DC))

        def rope_kv(b):
            pool.wait_ge(s_kv, 32 * b + 32)
            for lo, src in ((0, 32), (32, 0)):
                sink = ropek[:, 1, lo:lo + 32].unsqueeze(1).broadcast_to((P, SEQS, 32))
                pool.tensor_tensor(kt[:, :, lo:lo + 32], kv[:, :, src:src + 32], sink, ALU.mult).then_inc(s_kprod, 1)
            pool.wait_ge(s_kprod, 3 * b + 2)
            pool.tensor_tensor(kv[:], kv[:], cosk, ALU.mult).then_inc(s_kprod, 1)

        def diagonal(b):
            pool.wait_ge(s_kprod, 3 * b + 3)
            for h in range(2):
                r = slice(64 * h, 64 * h + 64)
                if h:
                    pool.wait_ge(s_bd, 2 * b + 1)
                pool.tensor_tensor(bd[r, :, 64 * h:64 * h + 64], kv[r], kt[r], ALU.add).then_inc(s_bd, 1)
            pool.wait_ge(s_bd, 2 * b + 2)

        def linear(b):
            rope_kv(b)
            diagonal(b)

        def pairs(b, later, following):
            if later:
                pool.wait_ge(s_uo, 4 * b)
            for p in range(PAIRS):
                for k in range(3):
                    pool.wait_ge(s_rp, 24 * b + 3 * p + k + 1)
                    if p >= 2 and k == 0:
                        pool.wait_ge(s_qr, 8 * b + p - 1)
                    pool.tensor_tensor(roped[:, p % 2, k], prod[:, 2 * k], prod[:, 2 * k + 1], ALU.add)\
                        .then_inc(s_rope, 1)

        def cross(b, following):
            if following:
                rope_kv(b + 1)
                pool.wait_ge(s_seqfree, b + 1)
                diagonal(b + 1)
            else:
                for n in range(LAST):
                    y_lo_out(pool, n)
                    if n == 0:
                        f_lo_out(pool, 0, 0)

        over_blocks(pool, linear, pairs, cross)
        ffn_pool(pool)

    @block.scalar
    def _(act):
        def squares(b):
            act.wait_ge(s_xb, 16 * b + 16)
            for t in range(TILES):
                act.activation(xn[:, t], xb[:, t], ACT.Square, accum_out=ss[:, t:t + 1]).then_inc(s_ss, 1)

        def xT_hi_out(b, m, s_in, s_done):
            act.wait_ge(s_in, 2 * b + m + 1)
            act.activation(xT_hi[:, m], bank((6, 7)[m]), ACT.Copy).then_inc(s_done, 1)

        def tanh(b, i):
            act.wait_ge(s_pj, 8 * b + i + 1)
            act.activation(qkgv[:, (0, 1, 2, 3, 6, 7, 4, 5)[i]], bank(6 + i % 2), ACT.Tanh, scale=0.5).then_inc(s_th, 1)

        def x2T_out(b, t, f):
            act.wait_ge(s_x2t, 4 * b + t + 1)
            if t == 0:
                act.wait_ge(s_kept, 32 * b + 1)
            act.activation(x2T[:, :, t * P:(t + 1) * P],
                           ps[:, f, 0:KC * P].rearrange("p (c s) -> p c s", c=KC), ACT.Copy).then_inc(s_x2T, 1)

        def bdT_out(b, i):
            act.wait_ge(s_bdt, 2 * b + i + 1)
            act.activation(bdT[:, 4 * i:4 * i + 4, :].rearrange("p s n -> p (s n)"), bank(KV_BANKS[i]), ACT.Copy)\
                .then_inc(s_bdT, 1)

        def a_hi_out(k):
            p, kc = k // KC, k % KC
            act.wait_ge(s_aps, k + 1)
            act.activation(a_hi[:, kc, p, :], ps[:, k % 4, 0:384], ACT.Copy).then_inc(s_ahi, 1)

        def linear(b):
            squares(b)

            def w_hi_out(i):
                act.wait_ge(s_raw0[i], 16)
                act.activation(w_hi[:, i], raw_w[i], ACT.Copy).then_inc(s_whi, 1)

            w_hi_out(0)
            xT_hi_out(b, 0, s_xt, s_xthi)
            xT_hi_out(b, 1, s_xt, s_xthi)
            for i in range(1, 4):
                w_hi_out(i)
            tanh(b, 0)
            tanh(b, 1)
            for p in range(PAIRS):
                act.wait_ge(s_mps, p + 1)
                act.activation(m_w[:, p, :], ps[:, 4 + p % 2, 0:384], ACT.Copy).then_inc(s_m, 1)
            for i in range(2, 6):
                tanh(b, i)
            for k in range(4):
                a_hi_out(k)
            tanh(b, 6)
            tanh(b, 7)
            for k in range(4, 16):
                a_hi_out(k)
            for i in range(PAIRS // 2):
                act.wait_ge(s_ups, i + 1)
                act.activation(u_w[:, 2 * i:2 * i + 2, :], bank(4 + i % 2).rearrange("p (r d) -> p r d", d=D), ACT.Copy)\
                    .then_inc(s_u, 1)
            xT_hi_out(b, 0, s_x1t, s_x1hi)
            xT_hi_out(b, 1, s_x1t, s_x1hi)
            bdT_out(b, 0)
            bdT_out(b, 1)

        def pairs(b, later, following):
            act.wait_ge(s_x1, 4 * b + 4)
            if later:
                x2T_out(b - 1, 2, 6)
            else:
                act.activation(x1[:], xn[:], ACT.Copy).then_inc(s_x1c, 1)
            for p in range(PAIRS):
                act.wait_ge(s_qr, 8 * b + p + 1)
                act.activation(lq[:, p], bank(6 + p % 2), ACT.Copy).then_inc(s_lq, 1)
                if later and p == 0:
                    x2T_out(b - 1, 3, 7)
                    act.activation(x1[:], xn[:], ACT.Copy).then_inc(s_x1c, 1)
                    act.wait_ge(s_lsub, b)
                    act.activation(rt[:, 1], rt[:, 0], ACT.Exp).then_inc(s_lexp, 1)
                if following and p == 1:
                    act.wait_ge(s_x1c, b + 1)
                    squares(b + 1)

        def cross(b, following):
            n = b + 1

            def expo(t):
                for i in range(2):
                    w = e[:, t % 2, i * 512:(i + 1) * 512]
                    act.wait_ge(s_sub, 8 * b + 2 * t + i + 1)
                    act.activation(w, w, ACT.Exp).then_inc(s_exp, 1)

            def turned(t):
                act.wait_ge(s_tp, 4 * b + t + 1)
                act.activation(at[:, t % 2], ps[:, 2:4, :].rearrange("p k (r s) -> p (k r) s", s=P), ACT.Copy)\
                    .then_inc(s_at, 1)

            def context(t):
                for h in range(2):
                    act.wait_ge(s_av, 8 * b + 2 * t + h + 1)
                    act.activation(ct[:, :, 64 * h:64 * h + 64], bank(4 + h).rearrange("p (r s) -> p r s", s=SEQ),
                                   ACT.Copy).then_inc(s_ct, 1)

            xout = lambda t: x2T_out(b, t, 5 if following else 7)
            if following:
                xT_hi_out(n, 0, s_xt, s_xthi)
                xT_hi_out(n, 1, s_xt, s_xthi)
                expo(0)
                tanh(n, 0)
                tanh(n, 1)
                turned(0)
                expo(1)
                tanh(n, 2)
                context(0)
                tanh(n, 3)
                expo(2)
                tanh(n, 4)
                turned(1)
                tanh(n, 5)
                context(1)
                tanh(n, 6)
                expo(3)
                tanh(n, 7)
                turned(2)
                context(2)
                xout(0)
                turned(3)
                xout(1)
                context(3)
                xT_hi_out(n, 0, s_x1t, s_x1hi)
                xT_hi_out(n, 1, s_x1t, s_x1hi)
                bdT_out(n, 0)
                bdT_out(n, 1)
            else:
                for m in range(LAST):
                    cT_out(act, m)
                expo(0)
                turned(0)
                expo(1)
                context(0)
                y_hi_out(act, 0)
                expo(2)
                turned(1)
                context(1)
                act.wait_ge(s_fload[0], 32)
                f_hi_out(act, 0, 0)
                turned(2)
                expo(3)
                context(2)
                f_hi_out(act, 0, 1)
                turned(3)
                f_hi_out(act, 0, 2)
                xout(0)
                context(3)
                xout(1)
                y_hi_out(act, 1)
                y_hi_out(act, 2)

        over_blocks(act, linear, pairs, cross)
        ffn_scalar(act, x2T_out)

    @block.vector
    def _(dve):
        own = Own(dve, s_own_v)
        bc = lambda x, n: x.unsqueeze(2).broadcast_to((P, x.shape[1], n))

        def norm_rows(src, t0, n, s_done):
            for t in range(t0, t0 + n):
                own.step(dve.bn_stats(stats[:, t, :], src[:, t]))
            own.need()
            for t in range(t0, t0 + n):
                own.step(dve.bn_aggr(mv[:, t, :], stats[:, t, :]))
            own.need()
            val, y, w = (nt[:, k, t0:t0 + n] for k in range(3))
            own.step(dve.tensor_scalar(val, mv[:, t0:t0 + n, 1], LN_EPS, None, ALU.add))
            if n == 1:
                own.step(dve.tensor_scalar(half, mv[:, t0:t0 + n, 1], LN_EPS, -0.5, ALU.add, ALU.mult))
            rsqrt(dve, own, val, y, w, half if n == 1 else None)
            own.need()
            for t in range(t0, t0 + n):
                dve.tensor_scalar(src[:, t], src[:, t], mv[:, t, 0:1], nt[:, 1, t:t + 1], ALU.subtract, ALU.mult)\
                    .then_inc(s_done, 1)

        def rms(b):
            dve.wait_ge(s_ss, 4 * b + 4)
            own.need()
            own.step(dve.tensor_scalar(nt[:, 0], ss, 1.0 / D, RMS_EPS, ALU.mult, ALU.add))
            rsqrt(dve, own, nt[:, 0], nt[:, 1], nt[:, 2])
            own.need()
            for t in range(TILES):
                dve.tensor_scalar(xn[:, t], xb[:, t], nt[:, 1, t:t + 1], None, ALU.mult).then_inc(s_xn, 1)

        def xT_lo_out(b, m, s_in, s_done):
            dve.wait_ge(s_in, 2 * b + m + 1)
            dve.tensor_tensor(xT_lo[:, m], bank(6 + m), xT_hi[:, m].bitcast(F32), ALU.subtract).then_inc(s_done, 1)

        def silu(b, i):
            dve.wait_ge(s_th, 8 * b + i + 1)
            dst = qkgv[:, (0, 1, 2, 3, 6, 7)[i]]
            dve.scalar_tensor_tensor(out=dst, in0=dst, scalar=1.0, in1=bank(6 + i % 2), op0=ALU.add, op1=ALU.mult)\
                .then_inc(s_pa, 1)

        def masked(b):
            dve.wait_ge(s_st, b + 1)
            dve.tensor_tensor(st[:].rearrange("p (t n) -> p t n", n=P), bank(6).rearrange("p (t n) -> p t n", n=P),
                              mask[:].unsqueeze(1).broadcast_to((P, TILES, P)), ALU.mult).then_inc(s_sm, 1)

        def gated(b, m):
            dve.wait_ge(s_ot, 2 * b + m + 1)
            dve.scalar_tensor_tensor(out=gT[:, m], in0=gT[:, m], scalar=1.0, in1=bank((7, 6)[m]),
                                     op0=ALU.add, op1=ALU.mult).then_inc(s_og, 1)

        def residual1(b, i):
            dve.wait_ge(s_y, 2 * b + i + 1)
            dve.scalar_tensor_tensor(
                out=xn[:, 2 * i:2 * i + 2], in0=bank(7 - i).rearrange("p (t n) -> p t n", n=D), scalar=1.0 / 16,
                in1=xb[:, 2 * i:2 * i + 2], op0=ALU.mult, op1=ALU.add).then_inc(s_r1, 1)

        def norm1(b):
            dve.wait_ge(s_r1, 2 * b + 2)
            own.need()
            norm_rows(xn, 0, TILES, s_x1)

        def a_lo_out(k):
            p, kc = k // KC, k % KC
            dve.wait_ge(s_ahi, k + 1)
            dve.tensor_tensor(a_lo[:, kc, p, :], ps[:, k % 4, 0:384], a_hi[:, kc, p, :].bitcast(F32), ALU.subtract)\
                .then_inc(s_alo, 1)

        def linear(b):
            rms(b)

            def w_lo_out(i):
                dve.wait_ge(s_whi, i + 1)
                dve.tensor_tensor(w_lo[:, i], raw_w[i], w_hi[:, i].bitcast(F32), ALU.subtract).then_inc(s_wlo, 1)

            w_lo_out(0)
            xT_lo_out(b, 0, s_xthi, s_xtlo)
            xT_lo_out(b, 1, s_xthi, s_xtlo)
            for i in range(1, 4):
                w_lo_out(i)
            for i in range(6):
                silu(b, i)
            for k in range(8):
                a_lo_out(k)
            dve.wait_ge(s_const, 3 * 16)
            masked(b)
            for k in range(8, 12):
                a_lo_out(k)
            gated(b, 0)
            gated(b, 1)
            for k in range(12, 16):
                a_lo_out(k)
            residual1(b, 0)
            residual1(b, 1)
            norm1(b)
            xT_lo_out(b, 0, s_x1hi, s_x1lo)
            xT_lo_out(b, 1, s_x1hi, s_x1lo)
            dve.wait_ge(s_tables, 4 * 16)
            own.step(dve.tensor_scalar(neg, alpha[:], 0.0, None, ALU.is_lt))
            own.restart()

        t64 = lambda ap: ap.rearrange("p (s n) -> p s n", n=SEQ)

        def times(dst, src, table, r=slice(0, P), o=slice(0, P)):
            return dve.tensor_tensor(
                t64(prod[o, dst, :]), t64(ps[r, src, :]),
                ropeq[r, table, :].unsqueeze(1).broadcast_to((r.stop - r.start, SEQS, SEQ)), ALU.mult)

        def pairs(b, later, following):
            own.need()
            for p in range(PAIRS):
                if following and p == 6:
                    rms(b + 1)
                f = 3 * (p % 2)
                for k in range(3):
                    if p >= 1:
                        dve.wait_ge(s_rope, 24 * b + 3 * p - 2 + k)
                    if k < 2:
                        dve.wait_ge(s_q, 24 * b + 3 * p + 2)
                        times(2 * k, f + k, 2 * k)
                        times(2 * k + 1, f + 1 - k, 2 * k + 1).then_inc(s_rp, 1)
                    else:
                        dve.wait_ge(s_q, 24 * b + 3 * p + 3)
                        times(4, f + 2, 4)
                        times(5, f + 2, 5, slice(64, 128), slice(0, 64))
                        times(5, f + 2, 5, slice(0, 64), slice(64, 128)).then_inc(s_rp, 1)
                if later and p == 0:
                    norm2(b - 1, 3)
                if later and p == 1:
                    shift_logits(b - 1, LOGITS)
                if later and 2 <= p < 5:
                    route(b - 1, 2 * p - 4)
                    route(b - 1, 2 * p - 3)
            own.restart()

        heads = lambda ap: ap.rearrange("p (h l) -> p h l", l=SEQ)

        def shift(b, t):
            if t == 0:
                dve.wait_ge(s_rope, 24 * b + 24)
            if t >= 2:
                dve.wait_ge(s_tp, 4 * b + t - 1)
            for i in range(2):
                dve.wait_ge(s_sc, 8 * b + 2 * t + i + 1)
                sc = heads(bank(i))
                m = mx[:, t % 2, 8 * i:8 * i + 8]
                own.need()
                own.step(dve.tensor_reduce(m, sc, AX, ALU.max))
                own.need()
                dve.tensor_tensor(heads(e[:, t % 2, i * 512:(i + 1) * 512]), sc, bc(m, SEQ), ALU.subtract)\
                    .then_inc(s_sub, 1)

        def normalise(b, t, halves=(0, 1)):
            for i in halves:
                dve.wait_ge(s_exp, 8 * b + 2 * t + i + 1)
                w = heads(e[:, t % 2, i * 512:(i + 1) * 512])
                own.need()
                own.step(dve.tensor_reduce(sm[:, 0, 8 * i:8 * i + 8], w, AX, ALU.add))
                own.need()
                own.step(dve.reciprocal(sm[:, 1, 8 * i:8 * i + 8], sm[:, 0, 8 * i:8 * i + 8]))
                own.need()
                dve.tensor_tensor(w, w, bc(sm[:, 1, 8 * i:8 * i + 8], SEQ), ALU.mult).then_inc(s_nrm, 1)

        def residual2(b, t, f):
            dve.wait_ge(s_uo, 4 * b + t + 1)
            if t == 0:
                dve.wait_ge(s_x1c, b + 1)
            dve.tensor_tensor(x1[:, t], ps[:, f, 0:D], x1[:, t], ALU.add).then_inc(s_r2, 1)

        def norm2(b, t):
            dve.wait_ge(s_r2, 4 * b + t + 1)
            own.need()
            norm_rows(x1, t, 1, s_x2)

        r0, r1, r2, r3 = (rt[:, k] for k in range(4))
        row = lambda k: rs[:, k, :]
        rb = lambda k: bc(row(k), EXPERTS)

        def tt(o, x, y, op):
            own.need()
            own.step(dve.tensor_tensor(o, x, y, op))

        def red(o, x, op):
            own.need()
            own.step(dve.tensor_reduce(o, x, AX, op))

        def shift_logits(b, place):
            lg = place.rearrange("p (t x) -> p t x", x=EXPERTS)
            dve.wait_ge(s_lg, b + 1)
            red(row(0), lg, ALU.max)
            own.need()
            dve.tensor_tensor(r0, lg, rb(0), ALU.subtract).then_inc(s_lsub, 1)

        def route(b, part):
            if part == 0:
                dve.wait_ge(s_lexp, b + 1)
                red(row(1), r1, ALU.add)
                own.need()
                own.step(dve.reciprocal(row(2), row(1)))
                tt(r0, r1, rb(2), ALU.mult)
            elif part == 1:
                own.need()
                for t in range(TILES):
                    own.step(dve.max(top[:, t, :], r0[:, t]))
                own.need()
                for t in range(TILES):
                    own.step(dve.match_replace(r1[:, t], top[:, t, :], r0[:, t], -1.0))
                own.need()
                own.step(dve.scalar_tensor_tensor(out=r2, in0=r1, scalar=0.0, in1=r0, op0=ALU.is_lt, op1=ALU.mult))
            elif part == 2:
                red(row(0), r2, ALU.add)
                own.step(dve.tensor_tensor(row(3), top[:, :, 7], neg.broadcast_to((P, TILES)), ALU.mult))
                own.step(dve.tensor_scalar(rs[:, 4, 0:1], neg, -1.0, 1.0, ALU.mult, ALU.add))
                own.need()
                own.step(dve.tensor_scalar(row(1), row(0), 1e-12, None, ALU.max))
                own.step(dve.scalar_tensor_tensor(out=row(3), in0=top[:, :, 0], scalar=rs[:, 4, 0:1], in1=row(3),
                                                  op0=ALU.mult, op1=ALU.add))
                own.need()
                own.step(dve.reciprocal(row(2), row(1)))
                own.step(dve.tensor_tensor(r1, r0, rb(3), ALU.is_equal))
                own.need()
                own.step(dve.tensor_tensor(r2, r2, rb(2), ALU.mult))
            elif part == 3:
                own.need()
                own.step(dve.tensor_tensor(r1, r1, rev_index[:].unsqueeze(1).broadcast_to((P, TILES, EXPERTS)),
                                           ALU.mult))
                red(row(5), r1, ALU.max)
                own.step(dve.tensor_scalar(r0, r2, alpha[:, 0:1], None, ALU.mult))
                tt(r1, r1, rb(5), ALU.is_equal)
                tt(r1, r1, r2, ALU.mult)
            elif part == 4:
                red(row(6), r0, ALU.max)
                own.need()
                own.step(dve.tensor_scalar(row(7), row(6), TAU, None, ALU.is_lt))
                own.step(dve.scalar_tensor_tensor(out=r2, in0=r0, scalar=TAU, in1=r2, op0=ALU.is_ge, op1=ALU.mult))
                tt(r1, r1, rb(7), ALU.mult)
                tt(r2, r2, r1, ALU.add)
            else:
                red(row(0), r2, ALU.add)
                own.need()
                own.step(dve.tensor_scalar(row(1), row(0), 1e-12, None, ALU.max))
                own.need()
                own.step(dve.reciprocal(row(2), row(1)))
                own.need()
                dve.wait_ge(s_kept, 32 * b + 1)
                dve.tensor_tensor(r3, r2, rb(2), ALU.mult).then_inc(s_c, 1)

        def cross(b, following):
            n = b + 1
            if following:
                xT_lo_out(n, 0, s_xthi, s_xtlo)
                xT_lo_out(n, 1, s_xthi, s_xtlo)
                shift(b, 0)
                normalise(b, 0)
                silu(n, 0)
                shift(b, 1)
                silu(n, 1)
                silu(n, 2)
                normalise(b, 1)
                silu(n, 3)
                shift(b, 2)
                silu(n, 4)
                residual2(b, 0, 4)
                normalise(b, 2)
                silu(n, 5)
                norm2(b, 0)
                shift(b, 3)
                residual2(b, 1, 4)
                normalise(b, 3, (0,))
                masked(n)
                normalise(b, 3, (1,))
                gated(n, 0)
                gated(n, 1)
                norm2(b, 1)
                residual1(n, 0)
                residual2(b, 2, 4)
                residual1(n, 1)
                norm1(n)
                xT_lo_out(n, 0, s_x1hi, s_x1lo)
                xT_lo_out(n, 1, s_x1hi, s_x1lo)
                residual2(b, 3, 4)
                norm2(b, 2)
            else:
                shift(b, 0)
                normalise(b, 0)
                shift(b, 1)
                normalise(b, 1)
                shift(b, 2)
                residual2(b, 0, 6)
                normalise(b, 2)
                shift(b, 3)
                residual2(b, 1, 6)
                normalise(b, 3)
                norm2(b, 0)
                norm2(b, 1)
                residual2(b, 2, 6)
                norm2(b, 2)
                residual2(b, 3, 6)
                norm2(b, 3)

        over_blocks(dve, linear, pairs, cross)
        ffn_vector(dve, own, shift_logits, route)

    @block.tensor
    def _(pe):
        def turn_x(b, m, s_in, s_done):
            for t in range(TILES):
                pe.wait_ge(s_in, 4 * b + t + 1)
                mm = pe.transpose(ps[:, 6 + m, t * P:(t + 1) * P], xn[:, t, m * P:(m + 1) * P], ident[:])
            mm.then_inc(s_done, 1)

        def projection(b, i):
            w, m = (0, 1, 2, 3)[i // 2], i % 2
            if i == 0:
                pe.wait_ge(s_xtlo, 2 * b + 2)
            if i >= 2:
                pe.wait_ge(s_pa, 6 * b + i - 1)
            if w == 2:
                for t in (2 * m, 2 * m + 1):
                    s = slice(t * P, (t + 1) * P)
                    for kc in range(KC):
                        mm = split_matmuls(pe, ps[:, 6 + m, (t % 2) * D:(t % 2 + 1) * D], xT_hi[:, kc, s],
                                           xT_lo[:, kc, s], w_hi[:, w, kc, :], w_lo[:, w, kc, :],
                                           kc == 0, kc == KC - 1)
            else:
                s = slice(m * P, (m + 1) * P)
                for kc in range(KC):
                    mm = split_matmuls(pe, bank(6 + m), w_hi[:, w, kc, s], w_lo[:, w, kc, s], xT_hi[:, kc, :],
                                       xT_lo[:, kc, :], kc == 0, kc == KC - 1)
            mm.then_inc(s_pj, 1)

        def self_scores(b):
            pe.wait_ge(s_th, 8 * b + 7)
            for t in range(TILES):
                s = slice(t * P, (t + 1) * P)
                for kc in range(KC):
                    mm = pe.matmul(ps[:, 6, s], kT[:, kc, s], qT[:, kc, s], start=kc == 0, stop=kc == KC - 1)
            mm.then_inc(s_st, 1)

        def self_context(b, m):
            if m == 0:
                pe.wait_ge(s_th, 8 * b + 8)
                pe.wait_ge(s_pa, 6 * b + 6)
                pe.wait_ge(s_sm, b + 1)
            for t in range(TILES):
                s = slice(t * P, (t + 1) * P)
                mm = pe.matmul(ps[:, 7 - m, s], v[:, t, m * P:(m + 1) * P], st[:, s], start=True, stop=True)
            mm.then_inc(s_ot, 1)

        def attn_out(b, i):
            pe.wait_ge(s_og, 2 * b + 2)
            for t in (2 * i, 2 * i + 1):
                for kc in range(KC):
                    mm = pe.matmul(ps[:, 7 - i, (t % 2) * D:(t % 2 + 1) * D], gT[:, kc, t * P:(t + 1) * P],
                                   wp[:, kc, :], start=kc == 0, stop=kc == KC - 1)
            mm.then_inc(s_y, 1)

        def turn_kv(b, i, f):
            pe.wait_ge(s_bd, 2 * b + 2)
            for q in range(4 * i, 4 * i + 4):
                mm = pe.transpose(ps[:, f, (q % 4) * P:(q % 4 + 1) * P], bd[:, q, :], ident[:])
            mm.then_inc(s_bdt, 1)

        def fold_m():
            pe.wait_ge(s_raw2, 8 * 16)
            for p in range(PAIRS):
                if p >= 2:
                    pe.wait_ge(s_m, p - 1)
                for t in range(3):
                    mm = pe.matmul(ps[:, 4 + p % 2, t * P:(t + 1) * P], l_qr[:, p, t, :], r_kr[:, p, :],
                                   start=True, stop=True)
                mm.then_inc(s_mps, 1)

        def fold_a(k0, k1):
            pe.wait_ge(s_raw1, 32)
            for k in range(k0, k1):
                p, kc = k // KC, k % KC
                if k >= 4:
                    pe.wait_ge(s_alo, k - 3)
                o = ps[:, k % 4, 0:384]
                l = [raw_wq[:, 2 * p + h, kc * P:(kc + 1) * P] for h in range(2)]
                w0 = raw_kcq[:, 2 * p, :].rearrange("p (g q) -> p g q", g=2)
                w1 = raw_kcq[:, 2 * p + 1, :].rearrange("p (g q) -> p g q", g=2)
                ab = o[:, 0:256].rearrange("p (g q) -> p g q", g=2)
                pe.matmul(ab[:, :, 0:96], l[0], w0, start=True, stop=True)
                pe.matmul(ab[:, :, 96:128], l[1], w1[:, :, 0:32], start=True, stop=True)
                pe.matmul(o[:, 256:384].rearrange("p (g q) -> p g q", g=2), l[1], w1[:, :, 32:96],
                          start=True, stop=True).then_inc(s_aps, 1)

        def fold_u():
            pe.wait_ge(s_raw3, 32)
            pe.wait_ge(s_m, PAIRS)
            for i in range(PAIRS // 2):
                if i >= 2:
                    pe.wait_ge(s_u, i - 1)
                for p in (2 * i, 2 * i + 1):
                    for h in range(2):
                        mm = pe.matmul(ps[64 * h:64 * h + 64, 4 + i % 2, (p % 2) * D:(p % 2 + 1) * D],
                                       raw_kv[:, 2 * p + h, :], raw_wo[:, 2 * p + h, :], start=True, stop=True)
                mm.then_inc(s_ups, 1)

        def turn_x2(b, t, f):
            pe.wait_ge(s_x2, 4 * b + t + 1)
            for m in range(KC):
                mm = pe.transpose(ps[:, f, m * P:(m + 1) * P], x1[:, t, m * P:(m + 1) * P], ident[:])
            mm.then_inc(s_x2t, 1)

        def logits(b, place):
            pe.wait_ge(s_x2T, 4 * b + 4)
            for t in range(TILES):
                for kc in range(KC):
                    mm = pe.matmul(place[:, t * EXPERTS:(t + 1) * EXPERTS], x2T[:, kc, t * P:(t + 1) * P],
                                   gate_w[:, kc, :], start=kc == 0, stop=kc == KC - 1)
            mm.then_inc(s_lg, 1)

        def linear(b):
            pe.wait_ge(s_ident, 16)
            turn_x(b, 0, s_xn, s_xt)
            turn_x(b, 1, s_xn, s_xt)
            pe.wait_ge(s_wlo, 1)
            projection(b, 0)
            projection(b, 1)
            fold_m()
            pe.wait_ge(s_wlo, 4)
            for i in range(2, 6):
                projection(b, i)
            fold_a(0, 4)
            projection(b, 6)
            projection(b, 7)
            fold_a(4, 8)
            self_scores(b)
            fold_a(8, 12)
            self_context(b, 0)
            self_context(b, 1)
            fold_a(12, 16)
            pe.wait_ge(s_const, 3 * 16)
            attn_out(b, 0)
            attn_out(b, 1)
            fold_u()
            turn_x(b, 0, s_x1, s_x1t)
            turn_x(b, 1, s_x1, s_x1t)
            pe.wait_ge(s_u, PAIRS // 2)
            pe.wait_ge(s_alo, PAIRS * KC)
            turn_kv(b, 0, KV_BANKS[0])
            turn_kv(b, 1, KV_BANKS[1])
            pe.wait_ge(s_tables, 4 * 16)
            pe.sem_inc(s_kept, 1)

        def pairs(b, later, following):
            def latent_q(p):
                if p == 0:
                    pe.wait_ge(s_bdT, 2 * b + 2)
                if p == 0 and later:
                    pe.wait_ge(s_x2T, 4 * b - 1)
                if p == 1 and later:
                    pe.wait_ge(s_lsub, b)
                if p >= 2:
                    pe.wait_ge(s_lq, 8 * b + p - 1)
                for k in range(3):
                    pe.wait_ge(s_rope, 24 * b + 3 * p + k + 1)
                    mm = pe.matmul(bank(6 + p % 2), m_w[:, p, k * P:(k + 1) * P], roped[:, p % 2, k, :],
                                   start=k == 0, stop=k == 2)
                mm.then_inc(s_qr, 1)

            pe.wait_ge(s_x1lo, 2 * b + 2)
            for p in range(PAIRS):
                if p == 1:
                    pe.wait_ge(s_bdT, 2 * b + 2)
                if later and p == 1:
                    turn_x2(b - 1, 2, 6)
                    pe.wait_ge(s_r2, 4 * b)
                    pe.wait_ge(s_ct, 8 * b)
                if p >= 2:
                    pe.wait_ge(s_rp, 24 * b + 3 * p - 3)
                for k in range(3):
                    s = slice(k * P, (k + 1) * P)
                    for kc in range(KC):
                        mm = split_matmuls(pe, bank(3 * (p % 2) + k), a_hi[:, kc, p, s], a_lo[:, kc, p, s],
                                           xT_hi[:, kc, :], xT_lo[:, kc, :], kc == 0, kc == KC - 1)
                    mm.then_inc(s_q, 1)
                if later and p == 2:
                    logits(b - 1, LOGITS)
                if p >= 1:
                    latent_q(p - 1)
                if later and p == 1:
                    turn_x2(b - 1, 3, 7)
            latent_q(PAIRS - 1)

        def cross(b, following):
            n = b + 1

            def scores(t):
                pe.wait_ge(s_rp, 24 * b + 24)
                for p in range(PAIRS):
                    if t >= 1 and p % 4 == 0:
                        pe.wait_ge(s_sub, 8 * b + 2 * t - 1 + p // 4)
                    if t == 0:
                        pe.wait_ge(s_lq, 8 * b + p + 1)
                    for h in range(2):
                        mm = pe.matmul(ps[64 * h:64 * h + 64, p // 4, (p % 4) * P:(p % 4 + 1) * P],
                                       lq[:, p, t * P + 64 * h:t * P + 64 * h + 64], bdT[:, 2 * t + h, :],
                                       start=True, stop=True)
                    if p % 4 == 3:
                        mm.then_inc(s_sc, 1)

            def turn(t):
                for p in range(PAIRS):
                    if p % 4 == 0:
                        pe.wait_ge(s_nrm, 8 * b + 2 * t + p // 4 + 1)
                    mm = pe.transpose(ps[:, 2 + p // 4, (p % 4) * P:(p % 4 + 1) * P], e[:, t % 2, p * P:(p + 1) * P],
                                      ident[:])
                mm.then_inc(s_tp, 1)

            def context(t):
                pe.wait_ge(s_at, 4 * b + t + 1)
                if following and t >= 1:
                    pe.wait_ge(s_r2, 4 * b + t)
                if not following and t == 0:
                    pe.wait_ge(s_cT, LAST)
                for h in range(2):
                    if following and t == 3 and h == 1:
                        pe.wait_ge(s_x2T, 4 * b + 2)
                    if not following and t >= 1:
                        pe.wait_ge(s_ct, 8 * b + 2 * t)
                    pe.matmul(bank(4 + h), bd[:, 2 * t + h, :], at[:, t % 2, :, 64 * h:64 * h + 64],
                              start=True, stop=True).then_inc(s_av, 1)

            def project(t):
                f = 4 if following else 6
                pe.wait_ge(s_ct, 8 * b + 2 * t + 2)
                if not following and t >= 1:
                    pe.wait_ge(s_r2, 4 * b + t)
                for p in range(PAIRS):
                    mm = pe.matmul(ps[:, f, 0:D], ct[:, p, :], u_w[:, p, :], start=p == 0, stop=p == PAIRS - 1)
                mm.then_inc(s_uo, 1)

            def xout(t):
                if following:
                    pe.wait_ge(s_ct, 8 * b + 6)
                if t >= 1:
                    pe.wait_ge(s_x2T, 4 * b + t)
                turn_x2(b, t, 5 if following else 7)

            if following:
                pe.wait_ge(s_lq, 8 * b + 7)
                turn_x(n, 0, s_xn, s_xt)
                pe.wait_ge(s_lq, 8 * b + 8)
                turn_x(n, 1, s_xn, s_xt)
                scores(0)
                projection(n, 0)
                projection(n, 1)
                scores(1)
                turn(0)
                projection(n, 2)
                context(0)
                projection(n, 3)
                scores(2)
                projection(n, 4)
                turn(1)
                project(0)
                projection(n, 5)
                context(1)
                projection(n, 6)
                scores(3)
                projection(n, 7)
                turn(2)
                project(1)
                self_scores(n)
                context(2)
                self_context(n, 0)
                self_context(n, 1)
                xout(0)
                turn(3)
                attn_out(n, 0)
                project(2)
                attn_out(n, 1)
                xout(1)
                context(3)
                pe.drain().then_inc(s_seqfree, 1)
                project(3)
                turn_x(n, 0, s_x1, s_x1t)
                turn_x(n, 1, s_x1, s_x1t)
                pe.wait_ge(s_at, 4 * b + 4)
                turn_kv(n, 0, KV_BANKS[0])
                pe.wait_ge(s_ct, 8 * b + 8)
                turn_kv(n, 1, KV_BANKS[1])
            else:
                pe.wait_ge(s_lq, 8 * b + 7)
                turn_c(pe, 0)
                pe.wait_ge(s_lq, 8 * b + 8)
                turn_c(pe, 1)
                pe.wait_ge(s_rp, 24 * b + 24)
                turn_c(pe, 2)
                scores(0)
                scores(1)
                turn(0)
                context(0)
                scores(2)
                turn(1)
                project(0)
                context(1)
                scores(3)
                turn(2)
                project(1)
                context(2)
                turn(3)
                project(2)
                xout(0)
                context(3)
                xout(1)
                project(3)

        over_blocks(pe, linear, pairs, cross)
        ffn_tensor(pe, turn_x2, logits)

    ctx.close()


def _constants():
    f = np.float32
    c = {"ident": np.eye(P, dtype=f)}
    j, i = np.arange(P)[:, None], np.arange(P)[None, :]
    c["mask"] = ((j // SEQ == i // SEQ) & (j <= i)).astype(f)

    def table(dim):
        inv = (f(1.0) / np.power(f(10000.0), np.arange(0, dim, 2, dtype=f) / f(dim))).astype(f)
        ang = np.repeat(np.arange(SEQ, dtype=f)[:, None] * inv[None, :], 2, axis=1)
        return np.sin(ang).astype(f), np.cos(ang).astype(f)

    sin, cos = table(DQ)
    up = np.r_[0:96, 0:32]
    cu = np.r_[32:96]
    c["ropeq"] = np.ascontiguousarray(np.stack([
        cos[:, up].T, -sin[:, up].T, cos[:, up + HALF].T, sin[:, up + HALF].T,
        np.concatenate([cos[:, cu], cos[:, cu + HALF]], 1).T,
        np.concatenate([sin[:, cu + HALF], -sin[:, cu]], 1).T], axis=1)).astype(f)
    sin, cos = table(DC)
    sin = np.concatenate([-sin[:, :32], sin[:, 32:]], 1)
    c["ropek"] = np.ascontiguousarray(np.tile(np.stack([cos, sin], axis=1), (2, 1, 1))).astype(f)
    c["rev_index"] = np.tile(np.arange(EXPERTS, 0, -1, dtype=f)[None], (P, 1))
    return c


def kernel(**inputs):
    import concourse.bacc as bacc
    from concourse.bass_utils import run_bass_kernel_spmd as run

    x = {k: np.asarray(v) for k, v in inputs.items()}
    tiles = lambda w: w.reshape(-1, P, w.shape[-1]).transpose(1, 0, 2)
    lay = {
        "x": x["x"].reshape(BLOCKS, TILES, P, D).transpose(0, 2, 1, 3),
        "ctx_512": x["ctx_512"].reshape(BLOCKS, SEQS, SEQ, DC).transpose(0, 2, 1, 3),
        **{n: tiles(x[n].T) for n in ("L0_attn_Wq", "L0_attn_Wk", "L0_attn_Wv", "L0_attn_Wg", "L0_attn_Wp",
                                      "L0_ffn_gate_weight", "L0_xattn_Wo")},
        "L0_xattn_Wq": tiles(x["L0_xattn_Wq"]),
        "L0_xattn_w_kc_q": x["L0_xattn_w_kc_q"].transpose(1, 0, 2),
        "L0_xattn_w_kc_kv": x["L0_xattn_w_kc_kv"].transpose(1, 0, 2),
        "L0_xattn_W_qr": x["L0_xattn_W_qr"].reshape(PAIRS, 2, DQ, 64).transpose(3, 0, 1, 2),
        "L0_xattn_W_kr": x["L0_xattn_W_kr"].reshape(PAIRS, 2, DC, 64).transpose(3, 0, 1, 2),
        "L0_ffn_gate_up_proj": x["L0_ffn_gate_up_proj"].reshape(GROUPS, GROUP, 2, ROWS, SHARE, KC, P)
                               .transpose(0, 6, 5, 2, 3, 1, 4).reshape(GROUPS, P, KC * 2 * GW),
        "L0_ffn_down_proj": x["L0_ffn_down_proj"].transpose(0, 2, 1).reshape(GROUPS, GROUP, ROWS, SHARE, D)
                            .transpose(0, 1, 3, 2, 4).reshape(GROUPS, P, ROWS * D),
        "L0_ffn_layer_alpha": x["L0_ffn_layer_alpha"].reshape(1, 1),
        **_constants(),
    }
    nc = bacc.Bacc("TRN2", target_bir_lowering=False, num_devices=1)
    arrays = {n: np.ascontiguousarray(v) for n, v in lay.items()}
    aps = {n: nc.dram_tensor("in_" + n, v.shape, mybir.dt.from_np(v.dtype), kind="ExternalInput").ap()
           for n, v in arrays.items()}
    out = nc.dram_tensor("out", (BLOCKS, P, TILES, D), F32, kind="ExternalOutput").ap()
    c_dram = nc.dram_tensor("routing", (GROUPS, GROUP, TOKENS), F32).ap()
    build(nc, aps, out, c_dram)
    got = run(nc, [{"in_" + n: v for n, v in arrays.items()}], core_ids=[0]).results[0]["out"]
    return np.ascontiguousarray(got.transpose(0, 2, 1, 3)).reshape(32, SEQ, D)
```
